# Optimizing a Trainium2 kernel written in Bass

```python
import numpy as np
import jax
import jax.numpy as jnp

def _softmax(x, axis=-1):
    return jax.nn.softmax(x, axis=axis)

def _gelu(x):
    return jax.nn.gelu(x, approximate=True)

def _silu(x):
    return jax.nn.silu(x)

def _sigmoid(x):
    return jax.nn.sigmoid(x)

def _layernorm(x, axis=-1, eps=1e-05):
    m = jnp.mean(x, axis=axis, keepdims=True)
    v = jnp.var(x, axis=axis, keepdims=True)
    return (x - m) / jnp.sqrt(v + eps)

def _scatter_add(tgt, idx, src, axis=0):
    return tgt.at[idx].add(src)

def _segment_sum(src, seg, n):
    return jax.ops.segment_sum(src, seg, n)
kernel_name = 'mk_hybrid_d1_jaxref_r8_c79df8'

def setup_inputs(seed: int=0):
    np.random.seed(seed)
    _w = jnp.asarray

    def _L0_attn_a_setup():
        import jax, jax.numpy as jnp
        import numpy as np
        BASE_THETA = 0.5
        K_DOP = 0.2
        K_NOR = 0.15
        K_SERO = 0.1
        DIM = 128
        key = jax.random.key(seed)
        ks = jax.random.split(key, 9)
        scale = 1.0 / np.sqrt(DIM)
        x = jax.random.normal(ks[0], (2, 256, DIM), dtype=jnp.float32)
        Wq = jax.random.normal(ks[1], (DIM, DIM), dtype=jnp.float32) * scale
        bq = jnp.zeros((DIM,), dtype=jnp.float32)
        Wk = jax.random.normal(ks[2], (DIM, DIM), dtype=jnp.float32) * scale
        bk = jnp.zeros((DIM,), dtype=jnp.float32)
        Wv = jax.random.normal(ks[3], (DIM, DIM), dtype=jnp.float32) * scale
        bv = jnp.zeros((DIM,), dtype=jnp.float32)
        Wo = jax.random.normal(ks[4], (DIM, DIM), dtype=jnp.float32) * scale
        bo = jnp.zeros((DIM,), dtype=jnp.float32)
        return {'x': x, 'Wq': Wq, 'bq': bq, 'Wk': Wk, 'bk': bk, 'Wv': Wv, 'bv': bv, 'Wo': Wo, 'bo': bo}
    _L0_attn_a_in = _L0_attn_a_setup()

    def _L0_attn_b_setup():
        import jax, jax.numpy as jnp
        import numpy as np
        N_HEAD = 16
        N_EMBD = 128
        D_HEAD = N_EMBD // N_HEAD
        key = jax.random.key(seed)
        ks = jax.random.split(key, 5)
        B, T, C = (4, 256, N_EMBD)
        s = 1.0 / np.sqrt(C)
        return {'x': jax.random.normal(ks[0], (B, T, C), dtype=jnp.float32), 'w_qkv': jax.random.normal(ks[1], (C, 3 * C), dtype=jnp.float32) * s, 'b_qkv': jnp.zeros((3 * C,), dtype=jnp.float32), 'w_out': jax.random.normal(ks[2], (C, C), dtype=jnp.float32) * s, 'b_out': jnp.zeros((C,), dtype=jnp.float32)}
    _L0_attn_b_in = _L0_attn_b_setup()

    def _L0_ffn_setup():
        import jax, jax.numpy as jnp
        import numpy as np
        N_HEADS = 4
        key = jax.random.key(seed)
        k1, k2, k3, k4 = jax.random.split(key, 4)
        dmodel, n_experts, expert_size = (128, 64, 128)
        B, S = (4, 256)
        x = jax.random.normal(k1, (B, S, dmodel), dtype=jnp.float32)
        expert_sel = jax.random.normal(k2, (n_experts, dmodel), dtype=jnp.float32) * dmodel ** (-0.5)
        keys = jax.random.normal(k3, (n_experts, dmodel, expert_size), dtype=jnp.float32) * dmodel ** (-0.5)
        values = jax.random.normal(k4, (n_experts, expert_size, dmodel), dtype=jnp.float32) * (n_experts * expert_size) ** (-0.5)
        return {'x': x, 'expert_sel': expert_sel, 'keys': keys, 'values': values}
    _L0_ffn_in = _L0_ffn_setup()
    _d = {'L0_attn_a_x': _L0_attn_a_in['x'], 'L0_attn_a_Wq': _L0_attn_a_in['Wq'], 'L0_attn_a_bq': _L0_attn_a_in['bq'], 'L0_attn_a_Wk': _L0_attn_a_in['Wk'], 'L0_attn_a_bk': _L0_attn_a_in['bk'], 'L0_attn_a_Wv': _L0_attn_a_in['Wv'], 'L0_attn_a_bv': _L0_attn_a_in['bv'], 'L0_attn_a_Wo': _L0_attn_a_in['Wo'], 'L0_attn_a_bo': _L0_attn_a_in['bo'], 'L0_attn_b_w_qkv': _L0_attn_b_in['w_qkv'], 'L0_attn_b_b_qkv': _L0_attn_b_in['b_qkv'], 'L0_attn_b_w_out': _L0_attn_b_in['w_out'], 'L0_attn_b_b_out': _L0_attn_b_in['b_out'], 'L0_ffn_expert_sel': _L0_ffn_in['expert_sel'], 'L0_ffn_keys': _L0_ffn_in['keys'], 'L0_ffn_values': _L0_ffn_in['values']}
    _x0 = _d['L0_attn_a_x']
    _d['L0_attn_a_x'] = jax.random.normal(jax.random.fold_in(jax.random.key(seed), 1), (2, 1024, 128), dtype=_x0.dtype)
    del _x0
    return _d

def reference(L0_attn_a_x, L0_attn_a_Wq, L0_attn_a_bq, L0_attn_a_Wk, L0_attn_a_bk, L0_attn_a_Wv, L0_attn_a_bv, L0_attn_a_Wo, L0_attn_a_bo, L0_attn_b_w_qkv, L0_attn_b_b_qkv, L0_attn_b_w_out, L0_attn_b_b_out, L0_ffn_expert_sel, L0_ffn_keys, L0_ffn_values):

    def _L0_attn_a_ref(x, Wq, bq, Wk, bk, Wv, bv, Wo, bo):
        import jax, jax.numpy as jnp
        import numpy as np
        BASE_THETA = 0.5
        K_DOP = 0.2
        K_NOR = 0.15
        K_SERO = 0.1
        DIM = 128
        q = jnp.einsum('bsd,ed->bse', x, Wq) + bq
        k = jnp.einsum('bsd,ed->bse', x, Wk) + bk
        v = jnp.einsum('bsd,ed->bse', x, Wv) + bv
        qk = jnp.einsum('bsd,btd->bst', q, k)
        theta = BASE_THETA + K_DOP * jax.nn.sigmoid(qk) + K_NOR * jnp.tanh(qk) + K_SERO * jax.nn.relu(qk)
        attn = jax.nn.softmax(theta, axis=-1)
        out = jnp.einsum('bst,btd->bsd', attn, v)
        return jnp.einsum('bsd,ed->bse', out, Wo) + bo

    def _L0_attn_b_ref(x, w_qkv, b_qkv, w_out, b_out):
        import jax, jax.numpy as jnp
        import numpy as np
        N_HEAD = 16
        N_EMBD = 128
        D_HEAD = N_EMBD // N_HEAD
        B, T, C = x.shape
        qkv = x @ w_qkv + b_qkv
        q, k, v = jnp.split(qkv, 3, axis=-1)

        def heads(t):
            return t.reshape(B, T, N_HEAD, D_HEAD).transpose(0, 2, 1, 3)
        q, k, v = (heads(q), heads(k), heads(v))
        scores = jnp.einsum('bhqd,bhkd->bhqk', q, k) / np.sqrt(D_HEAD)
        causal = jnp.tril(jnp.ones((T, T), dtype=bool))
        scores = jnp.where(causal, scores, -jnp.inf)
        probs = jax.nn.softmax(scores, axis=-1)
        out = jnp.einsum('bhqk,bhkd->bhqd', probs, v)
        out = out.transpose(0, 2, 1, 3).reshape(B, T, C)
        return out @ w_out + b_out

    def _L0_ffn_ref(x, expert_sel, keys, values):
        import jax, jax.numpy as jnp
        import numpy as np
        N_HEADS = 4
        B, S, d = x.shape
        n_experts = keys.shape[0]
        xf = x.reshape(-1, d)
        N = xf.shape[0]
        logits = xf @ expert_sel.T
        sel = jax.nn.sigmoid(logits)
        sel_val, sel_idx = jax.lax.top_k(sel, N_HEADS)
        gates = jnp.zeros((N, n_experts), dtype=x.dtype)
        gates = gates.at[jnp.arange(N)[:, None], sel_idx].set(sel_val)
        h = jnp.einsum('nd,kde->nke', xf, keys)
        scores = jax.nn.relu(h) * gates[:, :, None]
        out = jnp.einsum('nke,kev->nv', scores, values)
        return out.reshape(B, S, -1)
    x = L0_attn_a_x
    x = x + _L0_attn_a_ref(_layernorm(x, axis=-1), L0_attn_a_Wq, L0_attn_a_bq, L0_attn_a_Wk, L0_attn_a_bk, L0_attn_a_Wv, L0_attn_a_bv, L0_attn_a_Wo, L0_attn_a_bo)
    x = x + _L0_ffn_ref(_layernorm(x, axis=-1), L0_ffn_expert_sel, L0_ffn_keys, L0_ffn_values)
    x = x + _L0_attn_b_ref(_layernorm(x, axis=-1), L0_attn_b_w_qkv, L0_attn_b_b_qkv, L0_attn_b_w_out, L0_attn_b_b_out)
    x = x + _L0_ffn_ref(_layernorm(x, axis=-1), L0_ffn_expert_sel, L0_ffn_keys, L0_ffn_values)
    return x

_drawn_inputs = setup_inputs


def setup_inputs(seed=0):
    import zlib

    import numpy as np

    out = dict(_drawn_inputs(seed))
    spreads = {'L0_attn_a_bq': (0.0, 0.1),
     'L0_attn_a_bk': (0.0, 0.664),
     'L0_attn_a_bv': (0.0, 0.1),
     'L0_attn_a_bo': (0.0, 0.1),
     'L0_attn_b_b_qkv': (0.0, 0.1),
     'L0_attn_b_b_out': (0.0, 0.1)}
    factors = {}
    for name, (base, spread) in spreads.items():
        noise = np.random.default_rng([zlib.crc32(name.encode()), seed]).standard_normal(out[name].shape)
        drawn = base * np.exp(spread * noise) if base else spread * noise
        out[name] = jnp.asarray(drawn.astype(out[name].dtype))
    for name, factor in factors.items():
        out[name] = (out[name] * factor).astype(out[name].dtype)
    return out
```

```python
from contextlib import ExitStack

import concourse.bass as bass
from concourse import mybir

P = 128
ALU = mybir.AluOpType
ACT = mybir.ActivationFunctionType
AX = mybir.AxisListType.X
F32 = mybir.dt.float32
BF16 = mybir.dt.bfloat16
I32 = mybir.dt.int32
U32 = mybir.dt.uint32

TOP = 4
HEADS = 16
DH = 8
NEG = -1e30
LN_EPS = 1e-5
K_SIG, K_TANH, K_RELU = 0.2, 0.15, 0.1
SAT = 17.5


def hybrid_kernel(nc, x_in, Wq, bq, Wk, bk, Wv, bv, Wo, bo, w_qkv, b_qkv, w_out, b_out,
                  expert_sel, keys, values, out):
    B, T, D = x_in.shape
    E, _, F = keys.shape
    NT = T // P
    assert D == P and F == P and NT == 8 and E == 64 and B == 2
    TILES = (T * TOP + E * (P - 1)) // P
    GT = 4
    GROUPS = -(-TILES // (2 * GT)) * 2
    SLOTS = GROUPS * GT * P
    HG = 4
    UNITS = HEADS // HG
    W = 512
    PARTS = 3
    BIAS0 = PARTS * PARTS * DH
    SC_B = DH ** -0.5

    x_v = x_in.rearrange("b (t p) d -> b p t d", p=P)
    out_v = out.rearrange("b (t p) d -> b p t d", p=P)
    xbuf = [nc.dram_tensor(f"expert_in{b}", [SLOTS, D], F32, kind="Internal").ap() for b in range(B)]
    ybuf = [nc.dram_tensor(f"expert_out{b}", [SLOTS, D], F32, kind="Internal").ap() for b in range(B)]
    qk_dram = nc.dram_tensor("qk_parts", [B, 2, PARTS, HEADS, DH, T], BF16, kind="Internal").ap()

    ctx = ExitStack()
    with ctx:
        def sb(name, shape, dt=F32):
            return ctx.enter_context(nc.sbuf_tensor(name, shape, dt))

        sems = {}

        def sem(name):
            if name not in sems:
                sems[name] = ctx.enter_context(nc.semaphore(name))
            return sems[name]

        keys_sb = sb("keys_sb", [P, E, F])
        vals_sb = sb("vals_sb", [P, E, D])
        x = sb("x_state", [P, B, NT, D])
        xn = sb("xn", [P, B, NT, D])
        xnT = sb("xnT", [P, T])
        ident = sb("ident", [P, P])
        identb = sb("identb", [P, P], BF16)
        before = sb("before", [P, P], BF16)
        upto = sb("upto", [P, P], BF16)
        onesb = sb("onesb", [P, P], BF16)
        mask_qk = sb("mask_qk", [P, P], BF16)
        mask_kq = sb("mask_kq", [P, P], BF16)
        iota_i = sb("iota_i", [P, P], I32)
        iota_f = sb("iota_f", [P, P])
        wT = sb("wT", [P, 5, P])
        wqkv = sb("wqkv", [P, 3 * D])
        wout = sb("wout", [P, D])
        bcol = sb("bcol", [P, 5])
        brow = sb("brow", [P, 3, D])
        st = sb("ln_stats", [P, NT, 6])
        mv = sb("ln_mv", [P, NT, 2])
        ve = sb("ln_var", [P, NT])
        hv = sb("ln_half", [P, NT])
        yi = sb("ln_seed", [P, NT], I32)
        yr = sb("ln_rstd", [P, NT])
        ya = sb("ln_tmp", [P, NT])
        lg = sb("logits", [P, NT, E])
        top = sb("top", [P, NT, 8])
        topi = sb("topi", [P, NT, 8], U32)
        topf = sb("topf", [P, NT, TOP])
        eg = sb("exp_gate", [P, NT, TOP])
        eg1 = sb("exp_gate1", [P, NT, TOP])
        gates = sb("gates", [P, B, NT, TOP])
        onehot = sb("onehot", [P, NT, TOP, E], BF16)
        mask = sb("mask", [P, NT, E], BF16)
        cnt_i = sb("cnt_i", [E, 1], I32)
        tls_i = sb("tiles_i", [E, 1], I32)
        tls = sb("tiles_f", [E, 1], BF16)
        tlsB = sb("tiles_b", [E, P], BF16)
        base = sb("base", [P, E])
        endt = sb("end_tile", [E, 1])
        cmp = sb("ended", [E, P], BF16)
        tile_expert = sb("tile_expert", [1, B, P], I32)
        pos = sb("pos", [P, NT, E])
        prod = sb("prod", [P, 2, NT, E])
        slot_f = sb("slot_f", [P, TOP, NT])
        slot = sb("slot", [P, B, TOP, NT], I32)
        xg = sb("xg", [P, 2, GT, D])
        xgT = sb("xgT", [P, 2, GT * P])
        wk = sb("wk", [P, 2, GT, F])
        hT = sb("hT", [P, 2, GT * P])
        wraw = hT[:].rearrange("p r n -> p (r n)")[:, 0:5 * P].rearrange("p (i n) -> p i n", i=5)
        yt = sb("yt", [P, 2, GT * D])
        yg = sb("yg", [P, TOP, NT, D])
        SCR = 15616
        scr = sb("attention", [P, SCR])
        at = [0]

        def part(n, dt=F32):
            k = n * (2 if dt == BF16 else 4) // 4
            v = scr[:, at[0]:at[0] + k]
            at[0] += k
            assert at[0] <= SCR, at[0]
            return v if dt == F32 else v.bitcast(dt)

        qT, kT, vT = part(T), part(T), part(T)
        vp = part(T).rearrange("p (t d) -> p t d", d=D)
        xb = part(T).rearrange("p (t d) -> p t d", d=D)
        th1 = part(2 * T).rearrange("p (r n) -> p r n", r=2)
        th2 = part(2 * T).rearrange("p (r n) -> p r n", r=2)
        pr = part(2 * T).rearrange("p (r n) -> p r n", r=2)
        pT = part(2 * T).rearrange("p (r n) -> p r n", r=2)
        mx, nb, rs, rr = part(NT), part(NT), part(NT), part(NT)
        at[0] = 0
        qst = part(2 * HG * T, BF16).rearrange("p (r h n) -> p r h n", r=2, h=HG)
        kst = part(2 * HG * T, BF16).rearrange("p (r h n) -> p r h n", r=2, h=HG)
        at_ring = at[0]
        pex = part(2 * HG * W).rearrange("p (r h n) -> p r h n", r=2, h=HG)
        at_after = at[0]
        at[0] = at_ring
        qk_parts = [[part(T, BF16) for _ in range(PARTS)] for _ in range(2)]
        rest = part(T)
        assert at[0] <= at_after
        at[0] = at_after
        vaug = part(NT * HEADS * (DH + 1)).rearrange("p (t h c) -> p t h c", t=NT, h=HEADS)
        att = part(NT * D).rearrange("p (t d) -> p t d", d=D)
        av_sb = part(W)
        mxp = part(2 * HG * NT).rearrange("p (c h t) -> p c h t", c=2, h=HG)
        mT = part(P)
        mparts = [part(P, BF16) for _ in range(PARTS)]
        rec = part(NT * HG).rearrange("p (t h) -> p t h", h=HG)
        zrow = part(P, BF16)
        q32, k32 = hT[:].rearrange("p r n -> p (r n)"), xgT[:].rearrange("p r n -> p (r n)")
        attT = pex[:, 0, 0:T // W, :].rearrange("p h n -> p (h n)")
        xb_b = k32.rearrange("p (t d) -> p t d", d=D)

        ps = ctx.enter_context(nc.psum_tensor("ps", [P, 8, W], F32))

        def banks(a, n=1):
            return ps[:, a:a + n, :].rearrange("p b n -> p (b n)")

        block = ctx.enter_context(nc.Block())

        PHASES = [("a", 0, 0), ("r", 0, 0), ("a", 0, 1), ("r", 0, 1), ("f", 0, 0), ("f", 0, 1),
                  ("c", 0, 0), ("b", 1, 0), ("r", 1, 0), ("c", 0, 1), ("b", 1, 1), ("r", 1, 1),
                  ("f", 1, 0), ("f", 1, 1), ("c", 1, 0), ("c", 1, 1)]
        WITH_BARRIER = [i for i, ph in enumerate(PHASES)]

        def leave(name):
            return sem(f"{name}_left")

        def enter(eng, name, i):
            if i:
                for other in ("pe", "act", "dve"):
                    if other != name:
                        eng.wait_ge(sem(f"{other}_left"), i)

        def norm_no(kind, L, b):
            return 2 * (2 * L + b) + (kind == "r")

        def inst(L, b):
            return 2 * L + b

        STEPS = [(c, kt) for c in range(T // W) for kt in range((c + 1) * W // P)]
        NS = len(STEPS)
        LAST = [s for s, (c, kt) in enumerate(STEPS) if kt == (c + 1) * W // P - 1]
        PIECES = [(h, qt, c) for h in range(HG) for qt in range(NT) for c in range(qt * P // W + 1)]
        PER = 5

        def pieces_of(s):
            return range(min(s * PER, len(PIECES)), min((s + 1) * PER, len(PIECES)))

        S_NEG = -(-len(PIECES) // PER)
        assert S_NEG + 1 < NS

        def step_cols(s):
            c, kt = STEPS[s]
            q0 = max(kt * P, c * W)
            return q0, (c + 1) * W - q0

        @block.sync
        def _(sp):
            for b in range(B):
                sp.dma_start(x[:, b], x_v[b]).then_inc(sem("x_loaded"), 16)
            for i, w in enumerate((Wq, Wk, Wv, Wo)):
                sp.dma_start(wraw[:, i, :], w).then_inc(sem("w_loaded"), 16)
            sp.dma_start(wraw[0:E, 4, :], expert_sel).then_inc(sem("w_loaded"), 16)
            for i, v in enumerate((bq, bk, bv, b_qkv[0:D], b_qkv[D:2 * D])):
                sp.dma_start(bcol[:, i:i + 1], v.rearrange("(p a) -> p a", a=1)).then_inc(sem("w_loaded"), 16)
            for i, v in enumerate((bo, b_qkv[2 * D:3 * D], b_out)):
                sp.dma_start(brow[:, i, :], v.rearrange("(a n) -> a n", a=1).to_broadcast([P, D])).then_inc(sem("w_loaded"), 16)
            sp.dma_start(wqkv[:], w_qkv).then_inc(sem("w_loaded"), 16)
            sp.dma_start(wout[:], w_out).then_inc(sem("w_loaded"), 16)
            sp.wait_ge(sem("yg_zeroed"), 1)
            for b in range(B):
                flat = xbuf[b].rearrange("(p r) d -> p (r d)", p=P)
                n = TOP * NT * D
                for c in range(SLOTS * D // P // n):
                    sp.dma_start(flat[:, c * n:(c + 1) * n], yg[:].rearrange("p j t d -> p (j t d)"),
                                 max_dma_last_dim=8192).then_inc(sem("xbuf_zeroed"), 16)
            for c in range(4):
                k = slice(c * E // 4, (c + 1) * E // 4)
                sp.dma_start(keys_sb[:, k, :], keys[k].rearrange("k d e -> d k e")).then_inc(sem("experts_loaded"), 16)
                sp.dma_start(vals_sb[:, k, :], values[k].rearrange("k e v -> e k v")).then_inc(sem("experts_loaded"), 16)

            def ffn(L, b):
                G0 = inst(L, b) * GROUPS
                xr = xbuf[b].rearrange("(g j p) d -> g p j d", j=GT, p=P)
                yr_ = ybuf[b].rearrange("(g j p) d -> g p j d", j=GT, p=P)
                sp.wait_ge(sem(f"scattered{b}"), 16 * TOP * NT * (L + 1))

                def load(g, r, late=True):
                    if late:
                        sp.wait_ge(sem("xg_used"), G0 + g - 1)
                    sp.dma_start(xg[:, r], xr[bass.ds(g, 1)].rearrange("a p j d -> (a p) j d")).then_inc(sem(f"xg_loaded{r}"), 16)

                def store(g, r):
                    sp.wait_ge(sem("y_ready"), G0 + g + 1)
                    sp.dma_start(yr_[bass.ds(g, 1)].rearrange("a p j d -> (a p) j d"),
                                 yt[:, r].rearrange("p (j d) -> p j d", j=GT)).then_inc(sem(f"y_stored{r}"), 16)
                load(0, 0, False)
                load(1, 1, False)
                with sp.Fori(1, GROUPS // 2) as i:
                    for r in range(2):
                        load(2 * i + r, r)
                        store(2 * i + r - 2, r)
                for g in (GROUPS - 2, GROUPS - 1):
                    store(g, g % 2)

            def attn_b(b):
                for i in range(2):
                    for p in range(PARTS):
                        sp.wait_ge(sem("part_ready"), (b * 2 + i) * PARTS + p + 1)
                        sp.dma_start(qk_dram[b, i, p].rearrange("h d n -> (h d) n"), qk_parts[i][p]).then_inc(sem("parts_stored"), 16)
                sp.wait_ge(sem("parts_stored"), 16 * 2 * PARTS * (b + 1))

                def load(u):
                    r, U = u % 2, b * UNITS + u
                    hs = slice(u * HG, (u + 1) * HG)
                    if u >= 2:
                        sp.wait_ge(sem("scores_issued"), HG * NS * (U - 1))
                    for i in range(PARTS):
                        for j in range(PARTS):
                            rows = slice((i * PARTS + j) * DH, (i * PARTS + j + 1) * DH)
                            sp.dma_start(qst[rows, r], qk_dram[b, 0, i, hs].rearrange("h d n -> d h n")).then_inc(sem(f"qk_loaded{r}"), 16)
                            sp.dma_start(kst[rows, r], qk_dram[b, 1, j, hs].rearrange("h d n -> d h n")).then_inc(sem(f"qk_loaded{r}"), 16)
                    sp.dma_start(qst[BIAS0:BIAS0 + PARTS, r].rearrange("p h (t q) -> p (h t) q", q=P),
                                 zrow[0:PARTS, :].unsqueeze(1).to_broadcast([PARTS, HG * NT, P])).then_inc(sem(f"qk_loaded{r}"), 16)

                def maxima(u):
                    r, U = u % 2, b * UNITS + u
                    sp.wait_ge(sem("max_parts"), U + 1)
                    for p in range(PARTS):
                        sp.dma_start(qst[BIAS0 + p:BIAS0 + p + 1, r].rearrange("a h (t q) -> a (h t) q", q=P),
                                     mparts[p][0:HG * NT, :]).then_inc(sem(f"max_loaded{r}"), 16)
                load(0)
                load(1)
                maxima(0)
                for u in range(1, UNITS):
                    maxima(u)
                    if u + 1 < UNITS:
                        load(u + 1)

            for i, (kind, L, b) in enumerate(PHASES):
                if kind == "f":
                    ffn(L, b)
                if kind == "b":
                    sp.wait_ge(sem("stacks_cleared"), 1)
                    attn_b(b)
                if kind == "c" and L == 1:
                    sp.wait_ge(sem("combined"), inst(L, b) + 1)
                    sp.dma_start(out_v[b], x[:, b]).then_inc(sem("out_stored"), 16)
            sp.wait_ge(sem("out_stored"), 16 * B)

        @block.gpsimd
        def _(pool):
            g = nc.gpsimd
            made = sem("const_made")
            g.memset(yg[:], 0.0).then_inc(sem("yg_zeroed"), 1)
            g.memset(ident[:], 0.0).then_inc(made, 1)
            g.memset(identb[:], 0.0).then_inc(made, 1)
            for m in (before, upto, onesb):
                g.memset(m[:], 1.0).then_inc(made, 1)
            g.memset(mask_qk[:], 0.0).then_inc(made, 1)
            g.memset(mask_kq[:], 0.0).then_inc(made, 1)
            pool.wait_ge(made, 7)
            for m, op, fill, cm in ((ident, ALU.not_equal, 1.0, 1), (identb, ALU.not_equal, 1.0, 1),
                                    (before, ALU.is_gt, 0.0, -1), (upto, ALU.is_ge, 0.0, -1),
                                    (mask_qk, ALU.is_ge, NEG, 1), (mask_kq, ALU.is_ge, NEG, -1)):
                g.affine_select(out=m[:], in_=m[:], compare_op=op, fill=fill, base=0,
                                pattern=[[-cm, P]], channel_multiplier=cm).then_inc(made, 1)
            g.iota(iota_i[:], pattern=[[1, P]], base=0, channel_multiplier=0).then_inc(made, 1)

            def attn_a(L, b):
                for i in range(NT):
                    n = b * NT + i
                    pool.wait_ge(sem("tanh_ready"), 2 * n + 1)
                    g.tensor_scalar(th1[:, i % 2], th1[:, i % 2], K_TANH / K_RELU, None, ALU.mult).then_inc(sem("tanh_scaled"), 1)

            def scatter(L, b):
                pool.wait_ge(sem("slots_ready"), inst(L, b) + 1)
                if L == 0:
                    pool.wait_ge(sem("xbuf_zeroed"), 16 * B * (SLOTS * D // P // (TOP * NT * D)))
                for t in range(NT):
                    for j in range(TOP):
                        g.indirect_dma_start(xbuf[b], bass.IndirectOffsetOnAxis(ap=slot[:, b, j, t:t + 1], axis=0),
                                             xn[:, b, t, :], None).then_inc(sem(f"scattered{b}"), 16)

            def gather(L, b):
                n = inst(L, b)
                for r in range(2):
                    pool.wait_ge(sem(f"y_stored{r}"), 16 * GROUPS // 2 * (n + 1))
                if n:
                    pool.wait_ge(sem("combined"), n)
                for j in range(TOP):
                    for t in range(NT):
                        g.indirect_dma_start(yg[:, j, t, :], None, ybuf[b],
                                             bass.IndirectOffsetOnAxis(ap=slot[:, b, j, t:t + 1], axis=0)).then_inc(sem("gathered"), 16)

            for kind, L, b in PHASES:
                if kind == "a":
                    attn_a(L, b)
                if kind == "r":
                    scatter(L, b)
                if kind == "f":
                    gather(L, b)

        @block.scalar
        def _(act):
            a = nc.scalar

            def norm(n):
                act.wait_ge(sem("xnT_ps"), 2 * n + 1)
                a.copy(xnT[:, 0:W], banks(4)).then_inc(sem("xnT_ready"), 1)

            def attn_a(b):
                act.wait_ge(sem("a_proj_ps"), 3 * b + 1)
                a.activation(qT, banks(0, 2), ACT.Identity, bias=bcol[:, 0:1]).then_inc(sem("a_proj"), 1)
                act.wait_ge(sem("a_proj_ps"), 3 * b + 3)
                a.activation(vT, banks(4, 2), ACT.Identity, bias=bcol[:, 2:3]).then_inc(sem("a_vT"), 1)

                def tanhs(i):
                    n, r = b * NT + i, i % 2
                    act.wait_ge(sem("a_scores"), n + 1)
                    if i >= 2:
                        act.wait_ge(sem("a_theta"), n - 1)
                    a.activation(th1[:, r], banks(2 * r, 2), ACT.Tanh).then_inc(sem("tanh_ready"), 1)
                    a.activation(th2[:, r], banks(2 * r, 2), ACT.Tanh, scale=0.5).then_inc(sem("tanh_ready"), 1)

                def probs(i):
                    n, r = b * NT + i, i % 2
                    act.wait_ge(sem("a_theta"), n + 1)
                    if i >= 2:
                        act.wait_ge(sem("a_pT_ps"), 2 * (n - 1))
                    a.activation(pr[:, r], th2[:, r], ACT.Exp, scale=K_RELU, bias=nb[:, i:i + 1],
                                 accum_out=rs[:, i:i + 1]).then_inc(sem("a_probs"), 1)

                def pT_evac(i):
                    n, r = b * NT + i, i % 2
                    act.wait_ge(sem("a_pT_ps"), 2 * n + 1)
                    if i >= 2:
                        act.wait_ge(sem("a_out_ps"), n - 1)
                    a.copy(pT[:, r, 0:W], banks(4)).then_inc(sem("a_pT"), 1)

                tanhs(0)
                for i in range(NT):
                    if i + 1 < NT:
                        tanhs(i + 1)
                    probs(i)
                    pT_evac(i)

            def route(L, b):
                n = inst(L, b)
                act.wait_ge(sem("top_ready"), n + 1)
                a.activation(eg[:], top[:, :, 0:TOP], ACT.Exp, scale=-1.0).then_inc(sem("gate_exp"), 1)

            def ffn(L, b):
                G0 = inst(L, b) * GROUPS

                def xT(g, r, late):
                    act.wait_ge(sem("xgT_ps"), G0 + g + 1)
                    if late:
                        act.wait_ge(sem("h_ps"), G0 + g - 1)
                    a.copy(xgT[:, r], banks(r)).then_inc(sem("xgT_ready"), 1)

                def y(g, r, late):
                    act.wait_ge(sem("y_ps"), G0 + g + 1)
                    if late is not None:
                        act.wait_ge(sem(f"y_stored{r}"), 16 * (inst(L, b) * GROUPS // 2) + 16 * late)
                    a.copy(yt[:, r], banks(4 + r)).then_inc(sem("y_ready"), 1)
                xT(0, 0, False)
                xT(1, 1, False)
                xT(2, 0, True)
                y(0, 0, None)
                xT(3, 1, True)
                y(1, 1, None)
                with act.Fori(2, GROUPS // 2) as i:
                    for r in range(2):
                        xT(2 * i + r, r, True)
                        y(2 * i + r - 2, r, i - 1)
                for g in (GROUPS - 2, GROUPS - 1):
                    y(g, g % 2, g // 2)

            def attn_b(b):
                act.wait_ge(sem("b_proj_ps"), 3 * b + 1)
                a.activation(q32, banks(0, 2), ACT.Identity, bias=bcol[:, 3:4]).then_inc(sem("b_q32"), 1)
                act.wait_ge(sem("b_proj_ps"), 3 * b + 2)
                a.activation(k32, banks(2, 2), ACT.Identity, bias=bcol[:, 4:5]).then_inc(sem("b_k32"), 1)
                for t in range(UNITS * NS):
                    s, n = t % NS, b * UNITS * NS + t
                    _, w = step_cols(s)
                    for h in range(HG):
                        act.wait_ge(sem("scores_issued"), HG * n + h + 1)
                        if t == 0 and h == 0:
                            act.wait_ge(sem("parts_stored"), 16 * 2 * PARTS * (b + 1))
                        if t >= 2 and h == 0:
                            act.wait_ge(sem("pv_done"), n - 1)
                        a.activation(pex[:, t % 2, h, 0:w], banks(h)[:, 0:w], ACT.Exp, scale=SC_B).then_inc(sem("b_exp"), 1)
                act.wait_ge(sem("attT_ps"), b + 1)
                a.copy(attT, banks(0, 2)).then_inc(sem("attT"), 1)

            for i, (kind, L, b) in enumerate(PHASES):
                enter(act, "act", i)
                if kind in "abr":
                    norm(norm_no(kind, L, b))
                {"a": lambda: attn_a(b), "b": lambda: attn_b(b), "r": lambda: route(L, b),
                 "f": lambda: ffn(L, b), "c": lambda: None}[kind]()
                act.drain().then_inc(leave("act"), 1)

        @block.vector
        def _(dve):
            v = nc.vector
            chain = [0]

            def link(ins):
                chain[0] += 1
                ins.then_inc(sem("dve_chain"), 1)
                dve.wait_ge(sem("dve_chain"), chain[0])

            dve.wait_ge(sem("const_made"), 14)
            v.tensor_copy(iota_f[:], iota_i[:]).then_inc(sem("iota_ready"), 1)
            for i in range(5):
                dve.wait_ge(sem("wT_ps"), i + 1)
                n = E if i == 4 else P
                v.tensor_copy(wT[:, i, 0:n], banks(i)[:, 0:n]).then_inc(sem("wT_ready"), 1)

            def norm(n, b):
                if n == 0:
                    dve.wait_ge(sem("x_loaded"), 16 * B)
                for t in range(NT):
                    ins = v.bn_stats(st[:, t, :], x[:, b, t, :])
                link(ins)
                for t in range(NT):
                    ins = v.bn_aggr(mv[:, t, :], st[:, t, :])
                link(ins)
                link(v.tensor_scalar(ve[:], mv[:, :, 1], LN_EPS, None, ALU.add))
                v.tensor_scalar(hv[:], ve[:], 0.5, None, ALU.mult)
                link(v.tensor_scalar(yi[:], ve[:].bitcast(I32), 1, None, ALU.arith_shift_right))
                link(v.tensor_scalar(yr[:].bitcast(I32), yi[:], -1.0, float(0x5F3759DF), ALU.mult, ALU.add))
                for _ in range(4):
                    link(v.tensor_tensor(ya[:], yr[:], yr[:], ALU.mult))
                    link(v.scalar_tensor_tensor(ya[:], ya[:], -1.0, hv[:], ALU.mult, ALU.mult))
                    link(v.scalar_tensor_tensor(yr[:], ya[:], 1.5, yr[:], ALU.add, ALU.mult))
                for t in range(NT):
                    v.tensor_scalar(xn[:, b, t, :], x[:, b, t, :], mv[:, t, 0:1], yr[:, t:t + 1],
                                    ALU.subtract, ALU.mult).then_inc(sem("xn_ready"), 1)
                dve.wait_ge(sem("xnT_ps"), 2 * n + 2)
                v.tensor_copy(xnT[:, W:T], banks(5)).then_inc(sem("xnT_ready"), 1)

            def attn_a(b):
                dve.wait_ge(sem("a_proj_ps"), 3 * b + 2)
                v.tensor_scalar(kT, banks(2, 2), bcol[:, 1:2], None, ALU.add).then_inc(sem("a_proj"), 1)
                v.tensor_tensor(xb, x[:, b], brow[:, 0:1, :].to_broadcast([P, NT, D]), ALU.add)
                dve.wait_ge(sem("a_vp_ps"), b + 1)
                link(v.tensor_copy(vp, banks(6, 2).rearrange("p (t d) -> p t d", d=D)))
                dve.sem_inc(sem("a_vp"), 1)

                def theta(i):
                    n, r = b * NT + i, i % 2
                    dve.wait_ge(sem("tanh_ready"), 2 * n + 2)
                    v.scalar_tensor_tensor(th2[:, r], banks(2 * r, 2), 0.0, th2[:, r], ALU.max, ALU.add).then_inc(sem("a_relu"), 1)
                    dve.wait_ge(sem("a_relu"), n + 1)
                    dve.wait_ge(sem("tanh_scaled"), n + 1)
                    link(v.tensor_tensor_reduce(out=th2[:, r], in0=th2[:, r], in1=th1[:, r], scale=1.0, scalar=-1e38,
                                                op0=ALU.add, op1=ALU.max, accum_out=mx[:, i:i + 1]))
                    v.tensor_scalar(nb[:, i:i + 1], mx[:, i:i + 1], -K_RELU, None, ALU.mult).then_inc(sem("a_theta"), 1)

                def pT_evac(i):
                    n, r = b * NT + i, i % 2
                    dve.wait_ge(sem("a_pT_ps"), 2 * n + 2)
                    v.tensor_copy(pT[:, r, W:T], banks(5)).then_inc(sem("a_pT"), 1)

                def finish(i):
                    n = b * NT + i
                    dve.wait_ge(sem("a_probs"), n + 1)
                    link(v.reciprocal(rr[:, i:i + 1], rs[:, i:i + 1]))
                    dve.wait_ge(sem("a_out_ps"), n + 1)
                    v.scalar_tensor_tensor(x[:, b, i, :], banks(6 + i % 2)[:, 0:D], rr[:, i:i + 1], xb[:, i, :],
                                           ALU.mult, ALU.add).then_inc(sem("a_done"), 1)

                theta(0)
                for i in range(NT):
                    if i + 1 < NT:
                        theta(i + 1)
                    pT_evac(i)
                    if i:
                        finish(i - 1)
                finish(NT - 1)
                dve.wait_ge(sem("a_done"), NT * (b + 1))

            def route(L, b):
                n = inst(L, b)
                dve.wait_ge(sem("logits_ps"), n + 1)
                link(v.tensor_scalar(lg[:], banks(6).rearrange("p (t e) -> p t e", e=E), SAT, None, ALU.min))
                for t in range(NT):
                    ins = v.max(top[:, t, :], lg[:, t, :])
                link(ins)
                dve.sem_inc(sem("top_ready"), 1)
                for t in range(NT):
                    ins = v.max_index(topi[:, t, :], top[:, t, :], lg[:, t, :])
                link(ins)
                link(v.tensor_copy(topf[:], topi[:, :, 0:TOP]))
                for t in range(NT):
                    ins = v.tensor_tensor(onehot[:, t], iota_f[:, 0:E].unsqueeze(1).to_broadcast([P, TOP, E]),
                                          topf[:, t, :].unsqueeze(2).to_broadcast([P, TOP, E]), ALU.is_equal)
                link(ins)
                with nc.allow_low_precision("sums of at most four zeros and ones"):
                    v.tensor_reduce(mask[:], onehot[:].rearrange("p t j e -> p t e j"), AX, ALU.add).then_inc(sem("mask_ready"), 1)
                dve.wait_ge(sem("gate_exp"), n + 1)
                link(v.tensor_scalar(eg1[:], eg[:], 1.0, None, ALU.add))
                v.reciprocal(gates[:, b], eg1[:])
                dve.wait_ge(sem("count_ps"), n + 1)
                link(v.tensor_scalar(cnt_i[:], ps[0:E, 0, 0:1], float(P - 1), None, ALU.add))
                link(v.tensor_scalar(tls_i[:], cnt_i[:], 7, None, ALU.arith_shift_right))
                link(v.tensor_copy(tls[:], tls_i[:]))
                v.tensor_copy(tlsB[:], tls[:].to_broadcast([E, P])).then_inc(sem("tiles_ready"), 1)
                dve.wait_ge(sem("base_ps"), n + 1)
                v.tensor_copy(endt[:], ps[0:E, 1, 0:1])
                link(v.tensor_scalar(base[:], ps[:, 2, 0:E], float(P), None, ALU.mult))
                v.tensor_scalar(cmp[:], iota_f[0:E, :], endt[:], None, ALU.is_ge).then_inc(sem("ended_ready"), 1)
                link(v.tensor_tensor(pos[:], banks(7).rearrange("p (t e) -> p t e", e=E),
                                     base[:].unsqueeze(1).to_broadcast([P, NT, E]), ALU.add))
                for j in range(TOP):
                    link(v.tensor_tensor(prod[:, j % 2], onehot[:, :, j, :], pos[:], ALU.mult))
                    ins = v.tensor_reduce(slot_f[:, j, :], prod[:, j % 2], AX, ALU.add)
                link(ins)
                v.tensor_copy(slot[:, b], slot_f[:]).then_inc(sem("slots_ready"), 1)
                dve.wait_ge(sem("expert_ps"), n + 1)
                v.tensor_scalar(tile_expert[:, b, :], ps[0:1, 3, 0:P], float(E - 1), None, ALU.min).then_inc(sem("tile_experts"), 1)

            def ffn(L, b):
                G0 = inst(L, b) * GROUPS
                dve.wait_ge(sem("tile_experts"), inst(L, b) + 1)
                dve.wait_ge(sem("experts_loaded"), 16 * 8)
                regs = [v.alloc_register(f"dve_expert{j}_{L}{b}") for j in range(GT)]

                def weights(g, r, late):
                    v.reg_load(regs, tile_expert[0:1, b, bass.ds(g * GT, GT)])
                    if late:
                        dve.wait_ge(sem("h_ps"), G0 + g - 1)
                    for j in range(GT):
                        ins = v.tensor_copy(wk[:, r, j:j + 1, :], keys_sb[:, bass.ds(dve.snap(regs[j], min_val=0, max_val=E - 1), 1), :])
                    ins.then_inc(sem("wk_ready"), 1)

                def relu(g, r, late):
                    dve.wait_ge(sem("h_ps"), G0 + g + 1)
                    if late:
                        dve.wait_ge(sem("y_ps"), G0 + g - 1)
                    v.tensor_scalar(hT[:, r], banks(2 + r), 0.0, None, ALU.max).then_inc(sem("hT_ready"), 1)
                weights(0, 0, False)
                weights(1, 1, False)
                relu(0, 0, False)
                weights(2, 0, True)
                relu(1, 1, False)
                weights(3, 1, True)
                with dve.Fori(1, GROUPS // 2 - 1) as i:
                    for r in range(2):
                        relu(2 * i + r, r, True)
                        weights(2 * i + r + 2, r, True)
                for g in (GROUPS - 2, GROUPS - 1):
                    relu(g, g % 2, True)
                for reg in regs:
                    v.free_register(reg)

            def combine(L, b):
                n = inst(L, b)
                dve.wait_ge(sem("gathered"), 16 * TOP * NT * (n + 1))
                for j in range(TOP):
                    if j:
                        dve.wait_ge(sem("combine_step"), NT * (n * TOP + j))
                    for t in range(NT):
                        v.scalar_tensor_tensor(x[:, b, t, :], yg[:, j, t, :], gates[:, b, t, j:j + 1], x[:, b, t, :],
                                               ALU.mult, ALU.add).then_inc(sem("combine_step"), 1)
                dve.wait_ge(sem("combine_step"), NT * TOP * (n + 1))
                dve.sem_inc(sem("combined"), 1)

            def attn_b(b):
                if b == 0:
                    for r in range(2):
                        v.memset(qst[:, r], 0.0)
                        v.memset(kst[:, r], 0.0)
                    v.memset(zrow, 0.0)
                    link(v.memset(vaug[:, :, :, DH:DH + 1], 1.0))
                    for r in range(2):
                        ins = v.memset(kst[64:96, r], 1.0)
                    link(ins)
                    dve.sem_inc(sem("stacks_cleared"), 1)
                dve.wait_ge(sem("b_proj_ps"), 3 * b + 3)
                v.tensor_tensor(vaug[:, :, :, 0:DH].rearrange("p t h d -> p t h d"),
                                banks(6, 2).rearrange("p (t h d) -> p t h d", t=NT, h=HEADS),
                                brow[:, 1, :].rearrange("p (h d) -> p h d", d=DH).unsqueeze(1).to_broadcast([P, NT, HEADS, DH]),
                                ALU.add).then_inc(sem("b_vaug"), 1)
                for i, (name, full) in enumerate((("b_q32", q32), ("b_k32", k32))):
                    dve.wait_ge(sem(name), b + 1)
                    hi, mid, lo = qk_parts[i]
                    for k, (dst, src) in enumerate(((hi, full), (mid, rest))):
                        link(v.tensor_copy(dst, src))
                        dve.sem_inc(sem("part_ready"), 1)
                        if k == 0:
                            link(v.tensor_tensor(rest, full, hi, ALU.subtract))
                    v.tensor_tensor(lo, rest, mid, ALU.subtract).then_inc(sem("part_ready"), 1)
                    dve.wait_ge(sem("part_ready"), (b * 2 + i + 1) * PARTS)
                link(v.tensor_tensor(xb_b, x[:, b], brow[:, 2:3, :].to_broadcast([P, NT, D]), ALU.add))

                def piece(u, k):
                    h, qt, c = PIECES[k]
                    n = (b * UNITS + u) * len(PIECES) + k
                    w = min(W, (qt + 1) * P - c * W)
                    dve.wait_ge(sem("max_ps"), n + 1)
                    v.reduce_max(mxp[:, c, h, qt:qt + 1], banks(5 + n % 2)[:, 0:w], AX).then_inc(sem("max_read"), 1)

                def negate(u):
                    U = b * UNITS + u
                    dve.wait_ge(sem("max_read"), (U + 1) * len(PIECES))
                    h2 = W // P
                    link(v.tensor_tensor(mxp[:, 0, :, h2:], mxp[:, 0, :, h2:], mxp[:, 1, :, h2:], ALU.max))
                    link(v.tensor_scalar(mxp[:, 0], mxp[:, 0], -1.0, None, ALU.mult))
                    dve.sem_inc(sem("max_ready"), 1)

                def max_split(u):
                    U = b * UNITS + u
                    dve.wait_ge(sem("maxT_ps"), U + 1)
                    if U:
                        dve.wait_ge(sem(f"max_loaded{(u - 1) % 2}"), 16 * PARTS * ((U - 1) // 2 + 1))
                    m = HG * NT
                    src = ps[0:m, 7, 0:P]
                    link(v.tensor_copy(mparts[0][0:m], src))
                    link(v.tensor_tensor(mT[0:m], src, mparts[0][0:m], ALU.subtract))
                    link(v.tensor_copy(mparts[1][0:m], mT[0:m]))
                    link(v.tensor_tensor(mparts[2][0:m], mT[0:m], mparts[1][0:m], ALU.subtract))
                    dve.sem_inc(sem("max_parts"), 1)

                for k in range(len(PIECES)):
                    piece(0, k)
                negate(0)
                max_split(0)
                for t in range(UNITS * NS + 4):
                    u, s = divmod(t, NS)
                    if u + 1 < UNITS:
                        for k in pieces_of(s):
                            piece(u + 1, k)
                        if s == S_NEG:
                            negate(u + 1)
                        if s == S_NEG + 1:
                            max_split(u + 1)
                    e = t - 1
                    if 0 <= e < UNITS * NS and e % NS in LAST:
                        n = b * UNITS * len(LAST) + (e // NS) * len(LAST) + LAST.index(e % NS)
                        dve.wait_ge(sem("pv_done"), b * UNITS * NS + e + 1)
                        if n:
                            dve.wait_ge(sem("avT_ps"), n)
                        v.tensor_copy(av_sb, banks(4)).then_inc(sem("av_ready"), 1)
                    e = t - 3
                    if 0 <= e < UNITS * NS and e % NS in LAST:
                        c = LAST.index(e % NS)
                        eu = e // NS
                        n = b * UNITS * len(LAST) + eu * len(LAST) + c
                        dve.wait_ge(sem("avT_ps"), n + 1)
                        q = W // P
                        src = banks(7).rearrange("p (t h c) -> p t h c", t=q, h=HG)
                        link(v.reciprocal(rec[:, 0:q, :], src[:, :, :, DH]))
                        dst = att[:, c * q:(c + 1) * q, eu * HG * DH:(eu + 1) * HG * DH].rearrange("p t (h d) -> p t h d", d=DH)
                        for k in range(q):
                            ins = v.tensor_tensor(dst[:, k], src[:, k, :, 0:DH],
                                                  rec[:, k, :].unsqueeze(2).to_broadcast([P, HG, DH]), ALU.mult)
                        ins.then_inc(sem("att_ready"), 1)
                dve.wait_ge(sem("b_out_ps"), b + 1)
                link(v.tensor_tensor(x[:, b], banks(2, 2).rearrange("p (t d) -> p t d", d=D), xb_b, ALU.add))

            for i, (kind, L, b) in enumerate(PHASES):
                enter(dve, "dve", i)
                if kind in "abr":
                    norm(norm_no(kind, L, b), b)
                {"a": lambda: attn_a(b), "b": lambda: attn_b(b), "r": lambda: route(L, b),
                 "f": lambda: ffn(L, b), "c": lambda: combine(L, b)}[kind]()
                dve.drain().then_inc(leave("dve"), 1)

        @block.tensor
        def _(pe):
            def mm(o, lhsT, rhs, start=True, stop=True, **kw):
                return nc.tensor.matmul(o, lhsT, rhs, start=start, stop=stop, **kw)

            pe.wait_ge(sem("const_made"), 14)
            pe.wait_ge(sem("w_loaded"), 16 * 15)
            for i in range(5):
                n = E if i == 4 else P
                nc.tensor.transpose(banks(i)[:, 0:n], wraw[0:n, i, :], ident[0:n, 0:n]).then_inc(sem("wT_ps"), 1)
            pe.wait_ge(sem("wT_ready"), 5)

            def norm(n, b):
                for t in range(NT):
                    pe.wait_ge(sem("xn_ready"), n * NT + t + 1)
                    ins = nc.tensor.transpose(banks(4, 2)[:, t * P:(t + 1) * P], xn[:, b, t, :], ident[:])
                    if t % 4 == 3:
                        ins.then_inc(sem("xnT_ps"), 1)
                pe.wait_ge(sem("xnT_ready"), 2 * (n + 1))

            def project(o, w):
                for c in range(T // W):
                    ins = mm(banks(o + c), w, xnT[:, c * W:(c + 1) * W])
                return ins

            def attn_a(b):
                for i in range(3):
                    project(2 * i, wT[:, i, :]).then_inc(sem("a_proj_ps"), 1)
                pe.wait_ge(sem("a_vT"), b + 1)
                for t in range(NT):
                    ins = mm(banks(6, 2)[:, t * D:(t + 1) * D], vT[:, t * P:(t + 1) * P], wT[:, 3, :])
                ins.then_inc(sem("a_vp_ps"), 1)

                def scores(i):
                    n = b * NT + i
                    if i == 0:
                        pe.wait_ge(sem("a_proj"), 2 * (b + 1))
                    if i >= 2:
                        pe.wait_ge(sem("tanh_ready"), 2 * (n - 1))
                        pe.wait_ge(sem("a_relu"), n - 1)
                    for c in range(2):
                        ins = mm(banks(2 * (i % 2) + c), qT[:, i * P:(i + 1) * P], kT[:, c * W:(c + 1) * W])
                    ins.then_inc(sem("a_scores"), 1)

                def transposes(i):
                    n = b * NT + i
                    pe.wait_ge(sem("a_probs"), n + 1)
                    if i:
                        pe.wait_ge(sem("a_pT"), 2 * n)
                    for k in range(NT):
                        ins = nc.tensor.transpose(banks(4, 2)[:, k * P:(k + 1) * P], pr[:, i % 2, k * P:(k + 1) * P], ident[:])
                        if k % 4 == 3:
                            ins.then_inc(sem("a_pT_ps"), 1)

                def product(i):
                    n = b * NT + i
                    pe.wait_ge(sem("a_pT"), 2 * (n + 1))
                    if i == 0:
                        pe.wait_ge(sem("a_vp"), b + 1)
                    if i >= 2:
                        pe.wait_ge(sem("a_done"), n - 1)
                    for k in range(NT):
                        ins = mm(banks(6 + i % 2)[:, 0:D], pT[:, i % 2, k * P:(k + 1) * P], vp[:, k, :], k == 0, k == NT - 1)
                    ins.then_inc(sem("a_out_ps"), 1)
                scores(0)
                scores(1)
                for i in range(NT):
                    transposes(i)
                    product(i)
                    if i + 2 < NT:
                        scores(i + 2)

            def route(L, b):
                n = inst(L, b)
                for t in range(NT):
                    ins = mm(banks(6)[:, t * E:(t + 1) * E], xnT[:, t * P:(t + 1) * P], wT[:, 4, 0:E])
                ins.then_inc(sem("logits_ps"), 1)
                pe.wait_ge(sem("mask_ready"), n + 1)
                for t in range(NT):
                    ins = mm(ps[0:E, 0, 0:1], mask[:, t, :], onesb[:, 0:1], t == 0, t == NT - 1)
                ins.then_inc(sem("count_ps"), 1)
                for t in range(NT):
                    o = banks(7)[:, t * E:(t + 1) * E]
                    mm(o, before[:], mask[:, t, :], True, t == 0)
                    for k in range(t):
                        mm(o, onesb[:], mask[:, k, :], False, k == t - 1)
                pe.wait_ge(sem("tiles_ready"), n + 1)
                mm(ps[0:E, 1, 0:1], upto[0:E, 0:E], tls[:])
                mm(ps[:, 2, 0:E], tlsB[:], before[0:E, 0:E]).then_inc(sem("base_ps"), 1)
                pe.wait_ge(sem("ended_ready"), n + 1)
                mm(ps[0:1, 3, 0:P], onesb[0:E, 0:1], cmp[:]).then_inc(sem("expert_ps"), 1)

            def ffn(L, b):
                m = inst(L, b)
                G0 = m * GROUPS
                pe.wait_ge(sem("tile_experts"), m + 1)
                pe.wait_ge(sem("experts_loaded"), 16 * 8)
                regs = [nc.tensor.alloc_register(f"pe_expert{j}_{L}{b}") for j in range(GT)]

                def xT(g, r, late, k):
                    pe.wait_ge(sem(f"xg_loaded{r}"), 16 * (m * GROUPS // 2) + 16 * k)
                    if late:
                        pe.wait_ge(sem("xgT_ready"), G0 + g - 1)
                    for j in range(GT):
                        ins = nc.tensor.transpose(banks(r)[:, j * P:(j + 1) * P], xg[:, r, j, :], ident[:])
                    ins.then_inc(sem("xgT_ps"), 1)
                    pe.wait_ge(sem("xgT_ps"), G0 + g + 1)
                    pe.sem_inc(sem("xg_used"), 1)

                def hidden(g, r, late):
                    pe.wait_ge(sem("xgT_ready"), G0 + g + 1)
                    pe.wait_ge(sem("wk_ready"), G0 + g + 1)
                    if late:
                        pe.wait_ge(sem("hT_ready"), G0 + g - 1)
                    for j in range(GT):
                        ins = mm(banks(2 + r)[:, j * P:(j + 1) * P], wk[:, r, j, :], xgT[:, r, j * P:(j + 1) * P])
                    ins.then_inc(sem("h_ps"), 1)

                def outputs(g, r, late):
                    nc.tensor.reg_load(regs, tile_expert[0:1, b, bass.ds(g * GT, GT)])
                    pe.wait_ge(sem("hT_ready"), G0 + g + 1)
                    if late:
                        pe.wait_ge(sem("y_ready"), G0 + g - 1)
                    for j in range(GT):
                        e = pe.snap(regs[j], min_val=0, max_val=E - 1)
                        ins = mm(banks(4 + r)[:, j * D:(j + 1) * D], hT[:, r, j * P:(j + 1) * P],
                                 vals_sb[:, bass.ds(e, 1), :].rearrange("p a d -> p (a d)"))
                    ins.then_inc(sem("y_ps"), 1)
                xT(0, 0, False, 1)
                xT(1, 1, False, 1)
                hidden(0, 0, False)
                xT(2, 0, True, 2)
                hidden(1, 1, False)
                outputs(0, 0, False)
                xT(3, 1, True, 2)
                hidden(2, 0, True)
                outputs(1, 1, False)
                with pe.Fori(2, GROUPS // 2) as i:
                    for r in range(2):
                        xT(2 * i + r, r, True, i + 1)
                        hidden(2 * i + r - 1, 1 - r, True)
                        outputs(2 * i + r - 2, r, True)
                hidden(GROUPS - 1, 1, True)
                outputs(GROUPS - 2, 0, True)
                outputs(GROUPS - 1, 1, True)
                for reg in regs:
                    nc.tensor.free_register(reg)

            def attn_b(b):
                project(0, wqkv[:, 0:D]).then_inc(sem("b_proj_ps"), 1)
                project(2, wqkv[:, D:2 * D]).then_inc(sem("b_proj_ps"), 1)
                for t in range(NT):
                    ins = mm(banks(6, 2)[:, t * D:(t + 1) * D], xnT[:, t * P:(t + 1) * P], wqkv[:, 2 * D:3 * D])
                ins.then_inc(sem("b_proj_ps"), 1)
                pe.wait_ge(sem("b_vaug"), b + 1)
                pe.wait_ge(sem("b_k32"), b + 1)
                LOADS = 2 * PARTS * PARTS + 1

                def piece(u, k):
                    h, qt, c = PIECES[k]
                    n = (b * UNITS + u) * len(PIECES) + k
                    if k == 0:
                        pe.wait_ge(sem(f"qk_loaded{u % 2}"), 16 * LOADS * ((b * UNITS + u) // 2 + 1))
                    w = min(W, (qt + 1) * P - c * W)
                    if n >= 2:
                        pe.wait_ge(sem("max_read"), n - 1)
                    o = banks(5 + n % 2)
                    diag = c == qt * P // W
                    ins = mm(o[:, 0:w], qst[:, u % 2, h, qt * P:(qt + 1) * P], kst[:, u % 2, h, c * W:c * W + w], True, not diag)
                    if diag:
                        ins = mm(o[:, w - P:w], identb[:], mask_qk[:], False, True)
                    ins.then_inc(sem("max_ps"), 1)

                def maxT(u):
                    U = b * UNITS + u
                    pe.wait_ge(sem("max_ready"), U + 1)
                    if U:
                        pe.wait_ge(sem("max_parts"), U)
                    q = b * UNITS * len(LAST) + (u * len(LAST) - 1 if u else 0)
                    if q > 0:
                        pe.wait_ge(sem("att_ready"), q)
                    nc.tensor.transpose(ps[0:HG * NT, 7, 0:P], mxp[:, 0].rearrange("p h t -> p (h t)"), ident[:]).then_inc(sem("maxT_ps"), 1)

                def score(t, h):
                    u, s = divmod(t, NS)
                    n = b * UNITS * NS + t
                    if s == 0 and h == 0:
                        pe.wait_ge(sem(f"max_loaded{u % 2}"), 16 * PARTS * ((b * UNITS + u) // 2 + 1))
                    if t:
                        pe.wait_ge(sem("b_exp"), HG * (n - 1) + h + 1)
                    c, kt = STEPS[s]
                    q0, w = step_cols(s)
                    diag = kt * P >= c * W
                    ins = mm(banks(h)[:, 0:w], kst[:, u % 2, h, kt * P:(kt + 1) * P], qst[:, u % 2, h, q0:q0 + w], True, not diag)
                    if diag:
                        ins = mm(banks(h)[:, 0:P], identb[:], mask_kq[:], False, True)
                    ins.then_inc(sem("scores_issued"), 1)

                def product(t):
                    u, s = divmod(t, NS)
                    n = b * UNITS * NS + t
                    c, kt = STEPS[s]
                    q0, w = step_cols(s)
                    pe.wait_ge(sem("b_exp"), HG * (n + 1))
                    if kt == 0:
                        k = (b * UNITS + u) * len(LAST) + c
                        if k:
                            pe.wait_ge(sem("av_ready"), k)
                    for h in range(HG):
                        ins = mm(ps[32 * h:32 * h + DH + 1, 4, q0 - c * W:q0 - c * W + w], vaug[:, kt, u * HG + h, :],
                                 pex[:, t % 2, h, 0:w], kt == 0, s in LAST, tile_position=(0, 32 * h), skip_group_check=True)
                    ins.then_inc(sem("pv_done"), 1)

                if b == 0:
                    mm(banks(4), qst_zero, kst_zero)
                for k in range(len(PIECES)):
                    piece(0, k)
                maxT(0)
                for t in range(UNITS * NS + 4):
                    u, s = divmod(t, NS)
                    for h in range(HG):
                        if t < UNITS * NS:
                            score(t, h)
                        if u + 1 < UNITS:
                            ks = pieces_of(s)
                            for k in ks[h * len(ks) // HG:(h + 1) * len(ks) // HG]:
                                piece(u + 1, k)
                    if 1 <= t <= UNITS * NS:
                        product(t - 1)
                    e = t - 3
                    if 0 <= e < UNITS * NS and e % NS in LAST:
                        n = b * UNITS * len(LAST) + (e // NS) * len(LAST) + LAST.index(e % NS)
                        pe.wait_ge(sem("av_ready"), n + 1)
                        if n:
                            pe.wait_ge(sem("att_ready"), n)
                        pe.wait_ge(sem("max_parts"), min(b * UNITS + e // NS + 1, (b + 1) * UNITS))
                        for k in range(W // P):
                            ins = nc.tensor.transpose(banks(7)[:, k * P:(k + 1) * P], av_sb[:, k * P:(k + 1) * P], ident[:])
                        ins.then_inc(sem("avT_ps"), 1)
                    if u + 1 < UNITS and s == S_NEG + 1:
                        maxT(u + 1)
                pe.wait_ge(sem("att_ready"), (b + 1) * UNITS * len(LAST))
                for t in range(NT):
                    ins = nc.tensor.transpose(banks(0, 2)[:, t * P:(t + 1) * P], att[:, t, :], ident[:])
                ins.then_inc(sem("attT_ps"), 1)
                pe.wait_ge(sem("attT"), b + 1)
                for t in range(NT):
                    ins = mm(banks(2, 2)[:, t * D:(t + 1) * D], attT[:, t * P:(t + 1) * P], wout[:])
                ins.then_inc(sem("b_out_ps"), 1)

            qst_zero, kst_zero = ident[:], xnT[:, 0:W]
            for i, (kind, L, b) in enumerate(PHASES):
                enter(pe, "pe", i)
                if kind in "abr":
                    norm(norm_no(kind, L, b), b)
                {"a": lambda: attn_a(b), "b": lambda: attn_b(b), "r": lambda: route(L, b),
                 "f": lambda: ffn(L, b), "c": lambda: None}[kind]()
                pe.drain().then_inc(leave("pe"), 1)


_INS = ['L0_attn_a_x', 'L0_attn_a_Wq', 'L0_attn_a_bq', 'L0_attn_a_Wk', 'L0_attn_a_bk', 'L0_attn_a_Wv', 'L0_attn_a_bv',
        'L0_attn_a_Wo', 'L0_attn_a_bo', 'L0_attn_b_w_qkv', 'L0_attn_b_b_qkv', 'L0_attn_b_w_out', 'L0_attn_b_b_out',
        'L0_ffn_expert_sel', 'L0_ffn_keys', 'L0_ffn_values']


def kernel(**inputs):
    import numpy as _np
    import concourse.bacc as _bacc
    from concourse import mybir as _mybir
    from concourse.bass_utils import run_bass_kernel_spmd as _run

    nc = _bacc.Bacc("TRN2", target_bir_lowering=False, num_devices=1)
    arrays, args = {}, []
    for name in _INS:
        a = _np.ascontiguousarray(inputs[name])
        arrays[f"in_{name}"] = a
        args.append(nc.dram_tensor(f"in_{name}", a.shape, _mybir.dt.from_np(a.dtype), kind="ExternalInput").ap())
    o = nc.dram_tensor("out_x", inputs['L0_attn_a_x'].shape, _mybir.dt.float32, kind="ExternalOutput").ap()
    hybrid_kernel(nc, *args, o)
    r = _run(nc, [arrays], core_ids=[0])
    return r.results[0]["out_x"]
```

```python
from contextlib import ExitStack

import concourse.bass as bass
from concourse import mybir

P = 128
ALU = mybir.AluOpType
ACT = mybir.ActivationFunctionType
AX = mybir.AxisListType.X
F32 = mybir.dt.float32
BF16 = mybir.dt.bfloat16
I32 = mybir.dt.int32
U32 = mybir.dt.uint32

TOP = 4
HEADS = 16
DH = 8
NEG = -1e30
LN_EPS = 1e-5
K_SIG, K_TANH, K_RELU = 0.2, 0.15, 0.1
SAT = 17.5


def hybrid_kernel(nc, x_in, Wq, bq, Wk, bk, Wv, bv, Wo, bo, w_qkv, b_qkv, w_out, b_out,
                  expert_sel, keys, values, out):
    B, T, D = x_in.shape
    E, _, F = keys.shape
    NT = T // P
    assert D == P and F == P and NT == 8 and E == 64 and B == 2
    TILES = (T * TOP + E * (P - 1)) // P
    GT = 4
    RING = 4
    GROUPS = -(-TILES // (RING * GT)) * RING
    SLOTS = GROUPS * GT * P
    HG = 4
    UNITS = HEADS // HG
    W = 512
    PARTS = 3
    BIAS0 = PARTS * PARTS * DH
    SC_B = DH ** -0.5

    x_v = x_in.rearrange("b (t p) d -> b p t d", p=P)
    out_v = out.rearrange("b (t p) d -> b p t d", p=P)
    STORES = 3 * PARTS - 1
    LOADS = 2 * PARTS + 1
    ALL = B * UNITS
    xbuf = [nc.dram_tensor(f"expert_in{b}", [SLOTS, D], F32, kind="Internal").ap() for b in range(B)]
    ybuf = [nc.dram_tensor(f"expert_out{b}", [SLOTS, D], F32, kind="Internal").ap() for b in range(B)]
    qk_dram = nc.dram_tensor("qk_parts", [B, 2, HEADS, 2 * PARTS - 1, DH, T], BF16, kind="Internal").ap()

    ctx = ExitStack()
    with ctx:
        def sb(name, shape, dt=F32):
            return ctx.enter_context(nc.sbuf_tensor(name, shape, dt))

        sems = {}

        def sem(name):
            if name not in sems:
                sems[name] = ctx.enter_context(nc.semaphore(name))
            return sems[name]

        keys_sb = sb("keys_sb", [P, E, F])
        vals_sb = sb("vals_sb", [P, E, D])
        x = sb("x_state", [P, B, NT, D])
        xn = sb("xn", [P, B, NT, D])
        xnT = sb("xnT", [P, T])
        ident = sb("ident", [P, P])
        identb = sb("identb", [P, P], BF16)
        before = sb("before", [P, P], BF16)
        upto = sb("upto", [P, P], BF16)
        onesb = sb("onesb", [P, P], BF16)
        mask_qk = sb("mask_qk", [P, P], BF16)
        mask_kq = sb("mask_kq", [P, P], BF16)
        iota_i = sb("iota_i", [P, P], I32)
        iota_f = sb("iota_f", [P, P])
        wT = sb("wT", [P, 5, P])
        wqkv = sb("wqkv", [P, 3 * D])
        wout = sb("wout", [P, D])
        bcol = sb("bcol", [P, 5])
        brow = sb("brow", [P, 3, D])
        st = sb("ln_stats", [P, NT, 6])
        mv = sb("ln_mv", [P, NT, 2])
        ve = sb("ln_var", [P, NT])
        hv = sb("ln_half", [P, NT])
        yi = sb("ln_seed", [P, NT], I32)
        yr = sb("ln_rstd", [P, NT])
        ya = sb("ln_tmp", [P, NT])
        lg = sb("logits", [P, NT, E])
        top = sb("top", [P, NT, 8])
        topi = sb("topi", [P, NT, 8], U32)
        topf = sb("topf", [P, NT, TOP])
        eg = sb("exp_gate", [P, NT, TOP])
        eg1 = sb("exp_gate1", [P, NT, TOP])
        gates = sb("gates", [P, B, NT, TOP])
        onehot = sb("onehot", [P, NT, TOP, E], BF16)
        mask = sb("mask", [P, NT, E], BF16)
        cnt_i = sb("cnt_i", [E, 1], I32)
        tls_i = sb("tiles_i", [E, 1], I32)
        tls = sb("tiles_f", [E, 1], BF16)
        tlsB = sb("tiles_b", [E, P], BF16)
        base = sb("base", [P, E])
        endt = sb("end_tile", [E, 1])
        cmp = sb("ended", [E, P], BF16)
        tile_expert = sb("tile_expert", [1, B, P], I32)
        pos = sb("pos", [P, NT, E])
        prod = sb("prod", [P, 2, NT, E])
        mask2 = prod[:, 0].rearrange("p t e -> p (t e)").bitcast(BF16).rearrange("p (t j e) -> p t j e", t=NT, j=2)
        slot_f = sb("slot_f", [P, TOP, NT])
        slot = sb("slot", [P, B, TOP, NT], I32)
        exp_a = sb("expert_bufs_a", [P, 4, GT * D])
        exp_b = sb("expert_bufs_b", [P, 4, GT * D])
        xg = [exp_a[:, r].rearrange("p (j d) -> p j d", d=D) for r in range(2)] + [prod[:, r].rearrange("p t e -> p (t e)").rearrange("p (j d) -> p j d", j=GT) for r in range(2)]
        xgT = exp_b[:, 0:2]
        wk = exp_b[:, 2:4].rearrange("p r (j f) -> p r j f", f=F)
        hT = sb("hT", [P, 2, GT * P])
        wraw = hT[:].rearrange("p r n -> p (r n)")[:, 0:5 * P].rearrange("p (i n) -> p i n", i=5)
        yt = [exp_a[:, 2 + r] for r in range(2)]
        oh_f = onehot[:].rearrange("p t j e -> p (t j e)").bitcast(F32)
        yt += [oh_f[:, r * GT * D:(r + 1) * GT * D] for r in range(2)]
        yg = sb("yg", [P, TOP, NT, D])
        SCR = 15104
        scr = sb("attention", [P, SCR])
        at = [0]

        def part(n, dt=F32):
            k = n * (2 if dt == BF16 else 4) // 4
            v = scr[:, at[0]:at[0] + k]
            at[0] += k
            assert at[0] <= SCR, at[0]
            return v if dt == F32 else v.bitcast(dt)

        qT, kT, vT = part(T), part(T), part(T)
        vp = part(T).rearrange("p (t d) -> p t d", d=D)
        xb = part(T).rearrange("p (t d) -> p t d", d=D)
        th1 = part(2 * T).rearrange("p (r n) -> p r n", r=2)
        th2 = part(2 * T).rearrange("p (r n) -> p r n", r=2)
        pr = part(2 * T).rearrange("p (r n) -> p r n", r=2)
        pT = part(2 * T).rearrange("p (r n) -> p r n", r=2)
        mx, nb, rs, rr = part(NT), part(NT), part(NT), part(NT)
        at[0] = 0
        qst2 = part(2 * HG * T, BF16).rearrange("p (r h n) -> p r h n", r=2, h=HG)
        kst2 = part(2 * HG * T, BF16).rearrange("p (r h n) -> p r h n", r=2, h=HG)
        stack3 = [e[:].rearrange("p r n -> p (r n)").bitcast(BF16).rearrange("p (h n) -> p h n", h=HG) for e in (exp_a, exp_b)]
        QRING = 3
        qst = [qst2[:, 0], qst2[:, 1], stack3[0]]
        kst = [kst2[:, 0], kst2[:, 1], stack3[1]]
        at_ring = at[0]
        pex = part(2 * HG * W).rearrange("p (r n) -> p r n", r=2)
        at_after = at[0]
        at[0] = at_ring
        qk_parts = [[part(T, BF16) for _ in range(PARTS)] for _ in range(2)]
        rest = part(T)
        assert at[0] <= at_after
        at[0] = at_after
        vaug_flat = part(B * NT * HEADS * (DH + 1)).rearrange("p (n c) -> p n c", c=DH + 1)
        vaug = vaug_flat.rearrange("p (b t h) c -> p b t h c", b=B, t=NT)
        att = yg[:, 0]
        av_sb = yg[:, 1, 0:W // D, :].rearrange("p t d -> p (t d)")
        mxp = part(2 * HG * NT).rearrange("p (c h t) -> p c h t", c=2, h=HG)
        mT = part(P)
        mparts = [part(P, BF16) for _ in range(PARTS)]
        rec = part(NT * HG).rearrange("p (t h) -> p t h", h=HG)
        zrow = part(P, BF16)
        q32, k32 = hT[:].rearrange("p r n -> p (r n)"), xgT.rearrange("p r n -> p (r n)")
        attT = pex[:, 0, 0:T]

        ps = ctx.enter_context(nc.psum_tensor("ps", [P, 8, W], F32))

        def banks(a, n=1):
            return ps[:, a:a + n, :].rearrange("p b n -> p (b n)")

        block = ctx.enter_context(nc.Block())

        PHASES = [("a", 0, 0), ("r", 0, 0), ("a", 0, 1), ("r", 0, 1), ("f", 0, 0), ("f", 0, 1),
                  ("c", 0, 0), ("p", 1, 0), ("m", 1, 0), ("c", 0, 1), ("p", 1, 1),
                  ("u", 1, 0), ("r", 1, 0), ("u", 1, 1), ("r", 1, 1),
                  ("f", 1, 0), ("f", 1, 1), ("c", 1, 0), ("c", 1, 1)]

        def leave(name):
            return sem(f"{name}_left")

        def enter(eng, name, i):
            if i:
                for other in ("pe", "act", "dve"):
                    if other != name:
                        eng.wait_ge(sem(f"{other}_left"), i)

        def norm_no(i):
            return sum(kind in "apr" for kind, _, _ in PHASES[:i])

        def inst(L, b):
            return 2 * L + b

        STEPS = [(1, kt) for kt in range(8)] + [(0, kt) for kt in range(4)]
        NS = len(STEPS)
        LAST = [s for s in range(NS) if s + 1 == NS or STEPS[s + 1][0] != STEPS[s][0]]

        def step_cols(s):
            c, kt = STEPS[s]
            q0 = max(kt * P, c * W)
            return q0, (c + 1) * W - q0

        def in_bank(w):
            return min(HG, W // w)

        def chunks(s):
            k = min(HG, 2 * in_bank(step_cols(s)[1]))
            return [range(h, h + k) for h in range(0, HG, k)]

        def chunks_before(s):
            return sum(len(chunks(k)) for k in range(s))
        NCH = chunks_before(NS)

        PIECES = []
        for qt in range(NT):
            for c in range(qt * P // W + 1):
                w = min(W, (qt + 1) * P - c * W)
                PIECES += [(range(h, h + in_bank(w)), qt, c, w) for h in range(0, HG, in_bank(w))]
        NP = len(PIECES)
        FEED = range(0, 9)
        S_NEG = FEED[-1]

        def pieces_of(s):
            if s not in FEED:
                return range(0)
            cols = [step_cols(k)[1] for k in FEED]
            total = sum(len(hs) * w for hs, _, _, w in PIECES)
            at, acc = [0], 0
            for k in FEED:
                acc += step_cols(k)[1]
                n = at[-1]
                while n < NP and sum(len(hs) * w for hs, _, _, w in PIECES[:n + 1]) * sum(cols) <= acc * total:
                    n += 1
                at.append(n)
            at[-1] = NP
            return range(at[s - FEED[0]], at[s - FEED[0] + 1])

        @block.sync
        def _(sp):
            for b in range(B):
                sp.dma_start(x[:, b], x_v[b]).then_inc(sem("x_loaded"), 16)
            for i, w in enumerate((Wq, Wk, Wv, Wo)):
                sp.dma_start(wraw[:, i, :], w).then_inc(sem("w_loaded"), 16)
            sp.dma_start(wraw[0:E, 4, :], expert_sel).then_inc(sem("w_loaded"), 16)
            for i, v in enumerate((bq, bk, bv, b_qkv[0:D], b_qkv[D:2 * D])):
                sp.dma_start(bcol[:, i:i + 1], v.rearrange("(p a) -> p a", a=1)).then_inc(sem("w_loaded"), 16)
            for i, v in enumerate((bo, b_qkv[2 * D:3 * D], b_out)):
                sp.dma_start(brow[:, i, :], v.rearrange("(a n) -> a n", a=1).to_broadcast([P, D])).then_inc(sem("w_loaded"), 16)
            sp.dma_start(wqkv[:], w_qkv).then_inc(sem("w_loaded"), 16)
            sp.dma_start(wout[:], w_out).then_inc(sem("w_loaded"), 16)
            sp.wait_ge(sem("yg_zeroed"), 1)
            for b in range(B):
                flat = xbuf[b].rearrange("(p r) d -> p (r d)", p=P)
                n = TOP * NT * D
                for c in range(SLOTS * D // P // n):
                    sp.dma_start(flat[:, c * n:(c + 1) * n], yg[:].rearrange("p j t d -> p (j t d)"),
                                 max_dma_last_dim=8192).then_inc(sem("xbuf_zeroed"), 16)
            for c in range(4):
                k = slice(c * E // 4, (c + 1) * E // 4)
                sp.dma_start(keys_sb[:, k, :], keys[k].rearrange("k d e -> d k e")).then_inc(sem("experts_loaded"), 16)
                sp.dma_start(vals_sb[:, k, :], values[k].rearrange("k e v -> e k v")).then_inc(sem("experts_loaded"), 16)

            def ffn(L, b):
                G0 = inst(L, b) * GROUPS
                xr = xbuf[b].rearrange("(g j p) d -> g p j d", j=GT, p=P)
                sp.wait_ge(sem(f"scattered{b}"), 16 * TOP * NT * (L + 1))
                if b == 0:
                    sp.wait_ge(sem("routings_left"), L + 1)

                def load(g, r):
                    sp.dma_start(xg[r], xr[bass.ds(g, 1)].rearrange("a p j d -> (a p) j d")).then_inc(sem(f"xg_loaded{r}"), 16)
                for r in range(RING):
                    if b:
                        sp.wait_ge(sem("xgT_ps"), G0 + r - RING + 1)
                    load(r, r)
                with sp.Fori(1, GROUPS // RING) as i:
                    for r in range(RING):
                        sp.wait_ge(sem("xgT_ps"), G0 + RING * i + r - RING + 1)
                        load(RING * i + r, r)

            def store_parts(b):
                for i in range(2):
                    for p in range(PARTS):
                        sp.wait_ge(sem("part_ready"), (b * 2 + i) * PARTS + p + 1)
                        for k in range(p, 2 * PARTS - 1 if i else PARTS, PARTS):
                            sp.dma_start(qk_dram[b, i, :, k], qk_parts[i][p]).then_inc(sem("parts_stored"), 16)

            def load_unit(U):
                b, u = divmod(U, UNITS)
                r = U % QRING
                hs = slice(u * HG, (u + 1) * HG)
                if U >= QRING:
                    sp.wait_ge(sem("scores_issued"), NCH * (U - QRING + 1))
                for k in range(PARTS):
                    rows = slice(k * PARTS * DH, (k + 1) * PARTS * DH)
                    sp.dma_start(qst[r][rows], qk_dram[b, 0, hs, 0:PARTS].rearrange("h p d n -> (p d) h n")).then_inc(sem(f"qk_loaded{r}"), 16)
                    sp.dma_start(kst[r][rows], qk_dram[b, 1, hs, k:k + PARTS].rearrange("h p d n -> (p d) h n")).then_inc(sem(f"qk_loaded{r}"), 16)
                sp.dma_start(qst[r][BIAS0:BIAS0 + PARTS].rearrange("p h (t q) -> p (h t) q", q=P),
                             zrow[0:PARTS, :].unsqueeze(1).to_broadcast([PARTS, HG * NT, P])).then_inc(sem(f"qk_loaded{r}"), 16)

            def maxima(U):
                r = U % QRING
                sp.wait_ge(sem("max_parts"), U + 1)
                for p in range(PARTS):
                    sp.dma_start(qst[r][BIAS0 + p:BIAS0 + p + 1].rearrange("a h (t q) -> a (h t) q", q=P),
                                 mparts[p][0:HG * NT, :]).then_inc(sem(f"max_loaded{r}"), 16)

            for i, (kind, L, b) in enumerate(PHASES):
                if kind == "f":
                    ffn(L, b)
                if kind == "p":
                    store_parts(b)
                    sp.wait_ge(sem("parts_stored"), 16 * STORES * (b + 1))
                    if b == 0:
                        sp.wait_ge(sem("stacks_cleared"), 3)
                        load_unit(0)
                        load_unit(1)
                if kind == "m":
                    maxima(0)
                if kind == "u":
                    if b == 0:
                        sp.wait_ge(sem("stack3_cleared"), 2)
                    for U in range(b * UNITS, (b + 1) * UNITS):
                        if U + 2 < ALL:
                            load_unit(U + 2)
                        if U + 1 < ALL:
                            maxima(U + 1)
                if kind == "c" and L == 1:
                    sp.wait_ge(sem("combined"), inst(L, b) + 1)
                    sp.dma_start(out_v[b], x[:, b]).then_inc(sem("out_stored"), 16)
            sp.wait_ge(sem("out_stored"), 16 * B)

        @block.gpsimd
        def _(pool):
            g = nc.gpsimd
            made = sem("const_made")
            g.memset(yg[:], 0.0).then_inc(sem("yg_zeroed"), 1)
            g.memset(ident[:], 0.0).then_inc(made, 1)
            g.memset(identb[:], 0.0).then_inc(made, 1)
            for m in (before, upto, onesb):
                g.memset(m[:], 1.0).then_inc(made, 1)
            g.memset(mask_qk[:], 0.0).then_inc(made, 1)
            g.memset(mask_kq[:], 0.0).then_inc(made, 1)
            pool.wait_ge(made, 7)
            for m, op, fill, cm in ((ident, ALU.not_equal, 1.0, 1), (identb, ALU.not_equal, 1.0, 1),
                                    (before, ALU.is_gt, 0.0, -1), (upto, ALU.is_ge, 0.0, -1),
                                    (mask_qk, ALU.is_ge, NEG, 1), (mask_kq, ALU.is_ge, NEG, -1)):
                g.affine_select(out=m[:], in_=m[:], compare_op=op, fill=fill, base=0,
                                pattern=[[-cm, P]], channel_multiplier=cm).then_inc(made, 1)
            g.iota(iota_i[:], pattern=[[1, P]], base=0, channel_multiplier=0).then_inc(made, 1)

            def scatter(L, b):
                pool.wait_ge(sem("slots_ready"), inst(L, b) + 1)
                if L == 0:
                    pool.wait_ge(sem("xbuf_zeroed"), 16 * B * (SLOTS * D // P // (TOP * NT * D)))
                for t in range(NT):
                    for j in range(TOP):
                        g.indirect_dma_start(xbuf[b], bass.IndirectOffsetOnAxis(ap=slot[:, b, j, t:t + 1], axis=0),
                                             xn[:, b, t, :], None).then_inc(sem(f"scattered{b}"), 16)

            def gather(L, b):
                n = inst(L, b)
                for r in range(RING):
                    pool.wait_ge(sem(f"y_stored{r}"), 16 * (GROUPS // RING) * (n + 1))
                if n:
                    pool.wait_ge(sem("combined"), n)
                for j in range(TOP):
                    for t in range(NT):
                        g.indirect_dma_start(yg[:, j, t, :], None, ybuf[b],
                                             bass.IndirectOffsetOnAxis(ap=slot[:, b, j, t:t + 1], axis=0)).then_inc(sem(f"gathered{j}"), 16)

            def all_left(i):
                for other in ("pe", "act", "dve"):
                    pool.wait_ge(sem(f"{other}_left"), i)


            for i, (kind, L, b) in enumerate(PHASES):
                if (kind, L, b) == ("f", 0, 0):
                    all_left(i)
                    g.memset(zrow, 0.0).then_inc(sem("stack_zeroed"), 1)
                    g.memset(qst2.rearrange("p r h n -> p (r h n)").bitcast(F32), 0.0).then_inc(sem("stacks_cleared"), 1)
                    g.memset(kst2.rearrange("p r h n -> p (r h n)").bitcast(F32), 0.0).then_inc(sem("stack_zeroed"), 1)
                    g.memset(vaug_flat[:, :, DH:DH + 1], 1.0).then_inc(sem("stacks_cleared"), 1)
                    pool.wait_ge(sem("stack_zeroed"), 2)
                    pool.wait_ge(sem("stacks_cleared"), 2)
                    g.memset(kst2[64:96].rearrange("p r h n -> p (r h n)"), 1.0).then_inc(sem("stacks_cleared"), 1)
                    pool.wait_ge(sem("stacks_cleared"), 3)
                if kind == "u" and b == 0:
                    all_left(i)
                    g.memset(exp_a[:], 0.0).then_inc(sem("stack3_cleared"), 1)
                    g.memset(exp_b[:], 0.0).then_inc(sem("stack_zeroed"), 1)
                    pool.wait_ge(sem("stack_zeroed"), 3)
                    pool.wait_ge(sem("stack3_cleared"), 1)
                    g.memset(stack3[1][64:96], 1.0).then_inc(sem("stack3_cleared"), 1)
                    pool.wait_ge(sem("stack3_cleared"), 2)
                if kind == "r":
                    scatter(L, b)
                if kind == "f":
                    gather(L, b)

        @block.scalar
        def _(act):
            a = nc.scalar

            def norm(n):
                act.wait_ge(sem("xnT_ps"), 2 * n + 1)
                a.copy(xnT[:, 0:W], banks(4)).then_inc(sem("xnT_ready"), 1)

            def attn_a(b):
                act.wait_ge(sem("a_proj_ps"), 3 * b + 1)
                a.activation(qT, banks(0, 2), ACT.Identity, bias=bcol[:, 0:1]).then_inc(sem("a_proj"), 1)
                act.wait_ge(sem("a_proj_ps"), 3 * b + 3)
                a.activation(vT, banks(4, 2), ACT.Identity, bias=bcol[:, 2:3]).then_inc(sem("a_vT"), 1)

                def tanhs(i):
                    n, r = b * NT + i, i % 2
                    act.wait_ge(sem("a_scores"), n + 1)
                    if i >= 2:
                        act.wait_ge(sem("a_theta"), n - 1)
                    a.activation(th1[:, r], banks(2 * r, 2), ACT.Tanh).then_inc(sem("tanh_ready"), 1)
                    if i >= 2:
                        act.wait_ge(sem("a_probs"), n - 1)
                    a.activation(th2[:, r], banks(2 * r, 2), ACT.Tanh, scale=0.5).then_inc(sem("tanh_ready"), 1)

                def probs(i):
                    n, r = b * NT + i, i % 2
                    act.wait_ge(sem("a_theta"), n + 1)
                    if i >= 2:
                        act.wait_ge(sem("a_pT_ps"), 2 * (n - 1))
                    a.activation(pr[:, r], th2[:, r], ACT.Exp, scale=K_RELU, bias=nb[:, i:i + 1],
                                 accum_out=rs[:, i:i + 1]).then_inc(sem("a_probs"), 1)

                def pT_evac(i):
                    n, r = b * NT + i, i % 2
                    if i >= 2:
                        act.wait_ge(sem("a_out_ps"), n - 1)
                    for c in range(2):
                        act.wait_ge(sem("a_pT_ps"), 2 * n + c + 1)
                        a.copy(pT[:, r, c * W:(c + 1) * W], banks(4 + c)).then_inc(sem("a_pT"), 1)

                tanhs(0)
                tanhs(1)
                for i in range(NT):
                    probs(i)
                    if i + 2 < NT:
                        tanhs(i + 2)
                    pT_evac(i)

            def route(L, b):
                n = inst(L, b)
                act.wait_ge(sem("top_ready"), n + 1)
                a.activation(eg[:], top[:, :, 0:TOP], ACT.Exp, scale=-1.0).then_inc(sem("gate_exp"), 1)

            def ffn(L, b):
                G0 = inst(L, b) * GROUPS

                def xT(g, r, late):
                    act.wait_ge(sem("xgT_ps"), G0 + g + 1)
                    if late:
                        act.wait_ge(sem("h_ps"), G0 + g - 1)
                    a.copy(xgT[:, r], banks(r)).then_inc(sem("xgT_ready"), 1)

                yv = ybuf[b].rearrange("(g j p) d -> g p j d", j=GT, p=P)

                def y(g, r, k):
                    act.wait_ge(sem("y_ps"), G0 + g + 1)
                    if k is not None:
                        act.wait_ge(sem(f"y_stored{r}"), 16 * (inst(L, b) * (GROUPS // RING) + k))
                    a.copy(yt[r], banks(4 + r % 2)).then_inc(sem("y_ready"), 1)

                def store(g, r):
                    act.wait_ge(sem("y_ready"), G0 + g + 1)
                    act.dma_start(yv[bass.ds(g, 1)].rearrange("a p j d -> (a p) j d"),
                                  yt[r].rearrange("p (j d) -> p j d", j=GT)).then_inc(sem(f"y_stored{r}"), 16)
                first = 0 if inst(L, b) else None
                for g in range(RING + 2):
                    xT(g, g % 2, g >= 2)
                    if g >= 2:
                        y(g - 2, g - 2, first)
                        store(g - 2, g - 2)
                with act.Fori(1, GROUPS // RING - 1) as i:
                    for r in range(RING):
                        xT(RING * i + r + 2, r % 2, True)
                        y(RING * i + r, r, i)
                        store(RING * i + r, r)
                for g in range(GROUPS - RING, GROUPS):
                    if g + 2 < GROUPS:
                        xT(g + 2, g % 2, True)
                    y(g, g % RING, g // RING)
                    store(g, g % RING)

            def project_b(b):
                act.wait_ge(sem("b_proj_ps"), 3 * b + 1)
                a.activation(q32, banks(0, 2), ACT.Identity, bias=bcol[:, 3:4]).then_inc(sem("b_q32"), 1)
                act.wait_ge(sem("b_proj_ps"), 3 * b + 2)
                a.activation(k32, banks(2, 2), ACT.Identity, bias=bcol[:, 4:5]).then_inc(sem("b_k32"), 1)

            def units(b):
                for U in range(b * UNITS, (b + 1) * UNITS):
                    for s in range(NS):
                        w = step_cols(s)[1]
                        if U == 0 and s == 0:
                            act.wait_ge(sem("parts_stored"), 16 * STORES * B)
                        if U * NS + s >= 2:
                            act.wait_ge(sem("pv_done"), U * NS + s - 1)
                        for j, hs in enumerate(chunks(s)):
                            n = U * NCH + chunks_before(s) + j
                            act.wait_ge(sem("scores_issued"), n + 1)
                            k = min(len(hs), in_bank(w))
                            nb_ = len(hs) // k
                            a.activation(pex[:, s % 2, hs[0] * w:(hs[0] + len(hs)) * w].rearrange("p (b n) -> p b n", b=nb_),
                                         ps[:, 2 * (n % 2):2 * (n % 2) + nb_, 0:k * w], ACT.Exp, scale=SC_B).then_inc(sem("b_exp"), 1)
                act.wait_ge(sem("attT_ps"), b + 1)
                a.copy(attT, banks(0, 2)).then_inc(sem("attT"), 1)

            for i, (kind, L, b) in enumerate(PHASES):
                enter(act, "act", i)
                if kind in "apr":
                    norm(norm_no(i))
                {"a": lambda: attn_a(b), "p": lambda: project_b(b), "m": lambda: None, "u": lambda: units(b),
                 "r": lambda: route(L, b), "f": lambda: ffn(L, b), "c": lambda: None}[kind]()
                act.drain().then_inc(leave("act"), 1)

        @block.vector
        def _(dve):
            v = nc.vector
            chain = [0]

            def link(ins):
                chain[0] += 1
                ins.then_inc(sem("dve_chain"), 1)
                dve.wait_ge(sem("dve_chain"), chain[0])

            dve.wait_ge(sem("const_made"), 14)
            v.tensor_copy(iota_f[:], iota_i[:]).then_inc(sem("iota_ready"), 1)
            for i in range(5):
                dve.wait_ge(sem("wT_ps"), i + 1)
                n = E if i == 4 else P
                v.tensor_copy(wT[:, i, 0:n], banks(i)[:, 0:n]).then_inc(sem("wT_ready"), 1)

            def norm(n, b):
                if n == 0:
                    dve.wait_ge(sem("x_loaded"), 16 * B)
                for t in range(NT):
                    ins = v.bn_stats(st[:, t, :], x[:, b, t, :])
                link(ins)
                for t in range(NT):
                    ins = v.bn_aggr(mv[:, t, :], st[:, t, :])
                link(ins)
                link(v.tensor_scalar(ve[:], mv[:, :, 1], LN_EPS, None, ALU.add))
                v.tensor_scalar(hv[:], ve[:], 0.5, None, ALU.mult)
                link(v.tensor_scalar(yi[:], ve[:].bitcast(I32), 1, None, ALU.arith_shift_right))
                link(v.tensor_scalar(yr[:].bitcast(I32), yi[:], -1.0, float(0x5F3759DF), ALU.mult, ALU.add))
                for _ in range(3):
                    link(v.tensor_tensor(ya[:], yr[:], yr[:], ALU.mult))
                    link(v.scalar_tensor_tensor(ya[:], ya[:], -1.0, hv[:], ALU.mult, ALU.mult))
                    link(v.scalar_tensor_tensor(yr[:], ya[:], 1.5, yr[:], ALU.add, ALU.mult))
                for t in range(NT):
                    v.tensor_scalar(xn[:, b, t, :], x[:, b, t, :], mv[:, t, 0:1], yr[:, t:t + 1],
                                    ALU.subtract, ALU.mult).then_inc(sem("xn_ready"), 1)
                dve.wait_ge(sem("xnT_ps"), 2 * n + 2)
                v.tensor_copy(xnT[:, W:T], banks(5)).then_inc(sem("xnT_ready"), 1)

            def attn_a(b):
                dve.wait_ge(sem("a_proj_ps"), 3 * b + 2)
                v.tensor_scalar(kT, banks(2, 2), bcol[:, 1:2], None, ALU.add).then_inc(sem("a_proj"), 1)
                v.tensor_tensor(xb, x[:, b], brow[:, 0:1, :].to_broadcast([P, NT, D]), ALU.add)
                dve.wait_ge(sem("a_vp_ps"), b + 1)
                link(v.tensor_copy(vp, banks(6, 2).rearrange("p (t d) -> p t d", d=D)))
                dve.sem_inc(sem("a_vp"), 1)

                def theta(i):
                    n, r = b * NT + i, i % 2
                    dve.wait_ge(sem("tanh_ready"), 2 * n + 2)
                    v.scalar_tensor_tensor(th2[:, r], banks(2 * r, 2), 0.0, th2[:, r], ALU.max, ALU.add).then_inc(sem("a_relu"), 1)
                    dve.wait_ge(sem("a_relu"), n + 1)
                    link(v.scalar_tensor_tensor(th2[:, r], th1[:, r], K_TANH / K_RELU, th2[:, r], ALU.mult, ALU.add))
                    link(v.reduce_max(mx[:, i:i + 1], th2[:, r], AX))
                    v.tensor_scalar(nb[:, i:i + 1], mx[:, i:i + 1], -K_RELU, None, ALU.mult).then_inc(sem("a_theta"), 1)

                def finish(i):
                    n = b * NT + i
                    dve.wait_ge(sem("a_probs"), n + 1)
                    link(v.reciprocal(rr[:, i:i + 1], rs[:, i:i + 1]))
                    dve.wait_ge(sem("a_out_ps"), n + 1)
                    v.scalar_tensor_tensor(x[:, b, i, :], banks(6 + i % 2)[:, 0:D], rr[:, i:i + 1], xb[:, i, :],
                                           ALU.mult, ALU.add).then_inc(sem("a_done"), 1)

                theta(0)
                theta(1)
                for i in range(NT):
                    if i + 2 < NT:
                        theta(i + 2)
                    finish(i)
                dve.wait_ge(sem("a_done"), NT * (b + 1))

            def route(L, b):
                n = inst(L, b)
                dve.wait_ge(sem("logits_ps"), n + 1)
                link(v.tensor_scalar(lg[:], banks(6).rearrange("p (t e) -> p t e", e=E), SAT, None, ALU.min))
                for t in range(NT):
                    ins = v.max(top[:, t, :], lg[:, t, :])
                link(ins)
                dve.sem_inc(sem("top_ready"), 1)
                for t in range(NT):
                    ins = v.max_index(topi[:, t, :], top[:, t, :], lg[:, t, :])
                link(ins)
                link(v.tensor_copy(topf[:], topi[:, :, 0:TOP]))
                for t in range(NT):
                    ins = v.tensor_tensor(onehot[:, t], iota_f[:, 0:E].unsqueeze(1).to_broadcast([P, TOP, E]),
                                          topf[:, t, :].unsqueeze(2).to_broadcast([P, TOP, E]), ALU.is_equal)
                link(ins)
                link(v.tensor_tensor(mask2, onehot[:, :, 0:2, :], onehot[:, :, 2:4, :], ALU.add))
                v.tensor_tensor(mask[:], mask2[:, :, 0], mask2[:, :, 1], ALU.add).then_inc(sem("mask_ready"), 1)
                dve.wait_ge(sem("gate_exp"), n + 1)
                link(v.tensor_scalar(eg1[:], eg[:], 1.0, None, ALU.add))
                v.reciprocal(gates[:, b], eg1[:])
                dve.wait_ge(sem("count_ps"), n + 1)
                link(v.tensor_scalar(cnt_i[:], ps[0:E, 0, 0:1], float(P - 1), None, ALU.add))
                link(v.tensor_scalar(tls_i[:], cnt_i[:], 7, None, ALU.arith_shift_right))
                link(v.tensor_copy(tls[:], tls_i[:]))
                v.tensor_copy(tlsB[:], tls[:].to_broadcast([E, P])).then_inc(sem("tiles_ready"), 1)
                dve.wait_ge(sem("base_ps"), n + 1)
                v.tensor_copy(endt[:], ps[0:E, 1, 0:1])
                link(v.tensor_scalar(base[:], ps[:, 2, 0:E], float(P), None, ALU.mult))
                v.tensor_scalar(cmp[:], iota_f[0:E, :], endt[:], None, ALU.is_ge).then_inc(sem("ended_ready"), 1)
                link(v.tensor_tensor(pos[:], banks(7).rearrange("p (t e) -> p t e", e=E),
                                     base[:].unsqueeze(1).to_broadcast([P, NT, E]), ALU.add))
                for j in range(TOP):
                    link(v.tensor_tensor(prod[:, j % 2], onehot[:, :, j, :], pos[:], ALU.mult))
                    ins = v.tensor_reduce(slot_f[:, j, :], prod[:, j % 2], AX, ALU.add)
                link(ins)
                v.tensor_copy(slot[:, b], slot_f[:]).then_inc(sem("slots_ready"), 1)
                dve.wait_ge(sem("expert_ps"), n + 1)
                v.tensor_scalar(tile_expert[:, b, :], ps[0:1, 3, 0:P], float(E - 1), None, ALU.min).then_inc(sem("tile_experts"), 1)
                if b == B - 1:
                    dve.wait_ge(sem("tile_experts"), n + 1)
                    dve.sem_inc(sem("routings_left"), 1)

            def ffn(L, b):
                G0 = inst(L, b) * GROUPS
                dve.wait_ge(sem("tile_experts"), inst(L, b) + 1)
                dve.wait_ge(sem("experts_loaded"), 16 * 8)
                regs = [v.alloc_register(f"dve_expert{j}_{L}{b}") for j in range(GT)]

                def weights(g, r, late):
                    v.reg_load(regs, tile_expert[0:1, b, bass.ds(g * GT, GT)])
                    if late:
                        dve.wait_ge(sem("h_ps"), G0 + g - 1)
                    for j in range(GT):
                        ins = v.tensor_copy(wk[:, r, j:j + 1, :], keys_sb[:, bass.ds(dve.snap(regs[j], min_val=0, max_val=E - 1), 1), :])
                    ins.then_inc(sem("wk_ready"), 1)

                def relu(g, r, late):
                    dve.wait_ge(sem("h_ps"), G0 + g + 1)
                    if late:
                        dve.wait_ge(sem("y_ps"), G0 + g - 1)
                    v.tensor_scalar(hT[:, r], banks(2 + r), 0.0, None, ALU.max).then_inc(sem("hT_ready"), 1)
                weights(0, 0, False)
                weights(1, 1, False)
                relu(0, 0, False)
                weights(2, 0, True)
                relu(1, 1, False)
                weights(3, 1, True)
                with dve.Fori(1, GROUPS // 2 - 1) as i:
                    for r in range(2):
                        relu(2 * i + r, r, True)
                        weights(2 * i + r + 2, r, True)
                for g in (GROUPS - 2, GROUPS - 1):
                    relu(g, g % 2, True)
                for reg in regs:
                    v.free_register(reg)

            def combine(L, b):
                n = inst(L, b)
                for j in range(TOP):
                    dve.wait_ge(sem(f"gathered{j}"), 16 * NT * (n + 1))
                    if j:
                        dve.wait_ge(sem("combine_step"), NT * (n * TOP + j))
                    for t in range(NT):
                        v.scalar_tensor_tensor(x[:, b, t, :], yg[:, j, t, :], gates[:, b, t, j:j + 1], x[:, b, t, :],
                                               ALU.mult, ALU.add).then_inc(sem("combine_step"), 1)
                dve.wait_ge(sem("combine_step"), NT * TOP * (n + 1))
                dve.sem_inc(sem("combined"), 1)

            def project_b(b):
                if b == 0:
                    dve.wait_ge(sem("stacks_cleared"), 3)
                v.tensor_tensor(x[:, b], x[:, b], brow[:, 2:3, :].to_broadcast([P, NT, D]), ALU.add)
                if b:
                    dve.wait_ge(sem("parts_stored"), 16 * STORES * b)
                for i, (name, full) in enumerate((("b_q32", q32), ("b_k32", k32))):
                    dve.wait_ge(sem(name), b + 1)
                    hi, mid, lo = qk_parts[i]
                    for k, (dst, src) in enumerate(((hi, full), (mid, rest))):
                        link(v.tensor_copy(dst, src))
                        dve.sem_inc(sem("part_ready"), 1)
                        if k == 0:
                            link(v.tensor_tensor(rest, full, hi, ALU.subtract))
                    v.tensor_tensor(lo, rest, mid, ALU.subtract).then_inc(sem("part_ready"), 1)
                    dve.wait_ge(sem("part_ready"), (b * 2 + i + 1) * PARTS)
                dve.wait_ge(sem("b_proj_ps"), 3 * b + 3)
                v.tensor_tensor(vaug[:, b, :, :, 0:DH],
                                banks(6, 2).rearrange("p (t h d) -> p t h d", t=NT, h=HEADS),
                                brow[:, 1, :].rearrange("p (h d) -> p h d", d=DH).unsqueeze(1).to_broadcast([P, NT, HEADS, DH]),
                                ALU.add)

            def piece(U, k):
                hs, qt, c, w = PIECES[k]
                n = U * NP + k
                dve.wait_ge(sem("max_ps"), n + 1)
                v.reduce_max(mxp[:, c, hs[0]:hs[0] + len(hs), qt:qt + 1].rearrange("p h a -> p (h a)"),
                             banks(5 + n % 2)[:, 0:len(hs) * w].rearrange("p (h n) -> p h n", n=w), AX).then_inc(sem("max_read"), 1)

            def negate(U):
                dve.wait_ge(sem("max_read"), (U + 1) * NP)
                h2 = W // P
                link(v.tensor_tensor(mxp[:, 0, :, h2:], mxp[:, 0, :, h2:], mxp[:, 1, :, h2:], ALU.max))
                link(v.tensor_scalar(mxp[:, 0], mxp[:, 0], -1.0, None, ALU.mult))
                dve.sem_inc(sem("max_ready"), 1)

            def max_split(U):
                dve.wait_ge(sem("maxT_ps"), U + 1)
                if U:
                    dve.wait_ge(sem(f"max_loaded{(U - 1) % QRING}"), 16 * PARTS * ((U - 1) // QRING + 1))
                m = HG * NT
                src = ps[0:m, 7, 0:P]
                link(v.tensor_copy(mparts[0][0:m], src))
                link(v.tensor_tensor(mT[0:m], src, mparts[0][0:m], ALU.subtract))
                link(v.tensor_copy(mparts[1][0:m], mT[0:m]))
                link(v.tensor_tensor(mparts[2][0:m], mT[0:m], mparts[1][0:m], ALU.subtract))
                dve.sem_inc(sem("max_parts"), 1)

            def first_maxima():
                for k in range(NP):
                    piece(0, k)
                negate(0)
                max_split(0)

            def units(b):
                for t in range(UNITS * NS + 4):
                    u, s = divmod(t, NS)
                    U = b * UNITS + u
                    feeds = u < UNITS and U + 1 < ALL
                    if feeds:
                        for k in pieces_of(s):
                            piece(U + 1, k)
                        if s == S_NEG:
                            negate(U + 1)
                    e = t - 1
                    if 0 <= e < UNITS * NS and e % NS in LAST:
                        n = (b * UNITS + e // NS) * len(LAST) + LAST.index(e % NS)
                        dve.wait_ge(sem("pv_done"), b * UNITS * NS + e + 1)
                        if n:
                            dve.wait_ge(sem("avT_ps"), n)
                        v.tensor_copy(av_sb, banks(4)).then_inc(sem("av_ready"), 1)
                    e = t - 3
                    if 0 <= e < UNITS * NS and e % NS in LAST:
                        c = STEPS[e % NS][0]
                        eu = e // NS
                        n = (b * UNITS + eu) * len(LAST) + LAST.index(e % NS)
                        dve.wait_ge(sem("avT_ps"), n + 1)
                        q = W // P
                        src = banks(7).rearrange("p (t h c) -> p t h c", t=q, h=HG)
                        link(v.reciprocal(rec[:, 0:q, :], src[:, :, :, DH]))
                        dst = att[:, c * q:(c + 1) * q, eu * HG * DH:(eu + 1) * HG * DH].rearrange("p t (h d) -> p t h d", d=DH)
                        v.tensor_tensor(dst, src[:, :, :, 0:DH], rec[:, 0:q, :].unsqueeze(3).to_broadcast([P, q, HG, DH]),
                                        ALU.mult).then_inc(sem("att_ready"), 1)
                    if feeds and s == S_NEG + 1:
                        max_split(U + 1)
                dve.wait_ge(sem("b_out_ps"), b + 1)
                link(v.tensor_tensor(x[:, b], banks(2, 2).rearrange("p (t d) -> p t d", d=D), x[:, b], ALU.add))

            for i, (kind, L, b) in enumerate(PHASES):
                enter(dve, "dve", i)
                if kind in "apr":
                    norm(norm_no(i), b)
                {"a": lambda: attn_a(b), "p": lambda: project_b(b), "m": lambda: first_maxima(), "u": lambda: units(b),
                 "r": lambda: route(L, b), "f": lambda: ffn(L, b), "c": lambda: combine(L, b)}[kind]()
                dve.drain().then_inc(leave("dve"), 1)

        @block.tensor
        def _(pe):
            def mm(o, lhsT, rhs, start=True, stop=True, **kw):
                return nc.tensor.matmul(o, lhsT, rhs, start=start, stop=stop, **kw)

            pe.wait_ge(sem("const_made"), 14)
            pe.wait_ge(sem("w_loaded"), 16 * 15)
            for i in range(5):
                n = E if i == 4 else P
                nc.tensor.transpose(banks(i)[:, 0:n], wraw[0:n, i, :], ident[0:n, 0:n]).then_inc(sem("wT_ps"), 1)
            pe.wait_ge(sem("wT_ready"), 5)

            def norm(n, b):
                for t in range(NT):
                    pe.wait_ge(sem("xn_ready"), n * NT + t + 1)
                    ins = nc.tensor.transpose(banks(4, 2)[:, t * P:(t + 1) * P], xn[:, b, t, :], ident[:])
                    if t % 4 == 3:
                        ins.then_inc(sem("xnT_ps"), 1)
                pe.wait_ge(sem("xnT_ready"), 2 * (n + 1))

            def project(o, w):
                for c in range(T // W):
                    ins = mm(banks(o + c), w, xnT[:, c * W:(c + 1) * W])
                return ins

            def attn_a(b):
                for i in range(3):
                    project(2 * i, wT[:, i, :]).then_inc(sem("a_proj_ps"), 1)
                pe.wait_ge(sem("a_vT"), b + 1)
                for t in range(NT):
                    ins = mm(banks(6, 2)[:, t * D:(t + 1) * D], vT[:, t * P:(t + 1) * P], wT[:, 3, :])
                ins.then_inc(sem("a_vp_ps"), 1)

                def scores(i):
                    n = b * NT + i
                    if i == 0:
                        pe.wait_ge(sem("a_proj"), 2 * (b + 1))
                    if i >= 2:
                        pe.wait_ge(sem("tanh_ready"), 2 * (n - 1))
                        pe.wait_ge(sem("a_relu"), n - 1)
                    for c in range(2):
                        ins = mm(banks(2 * (i % 2) + c), qT[:, i * P:(i + 1) * P], kT[:, c * W:(c + 1) * W])
                    ins.then_inc(sem("a_scores"), 1)

                def transposes(i):
                    n = b * NT + i
                    pe.wait_ge(sem("a_probs"), n + 1)
                    if i:
                        pe.wait_ge(sem("a_pT"), 2 * n)
                    for k in range(NT):
                        ins = nc.tensor.transpose(banks(4, 2)[:, k * P:(k + 1) * P], pr[:, i % 2, k * P:(k + 1) * P], ident[:])
                        if k % 4 == 3:
                            ins.then_inc(sem("a_pT_ps"), 1)

                def product(i):
                    n = b * NT + i
                    pe.wait_ge(sem("a_pT"), 2 * (n + 1))
                    if i == 0:
                        pe.wait_ge(sem("a_vp"), b + 1)
                    if i >= 2:
                        pe.wait_ge(sem("a_done"), n - 1)
                    for k in range(NT):
                        ins = mm(banks(6 + i % 2)[:, 0:D], pT[:, i % 2, k * P:(k + 1) * P], vp[:, k, :], k == 0, k == NT - 1)
                    ins.then_inc(sem("a_out_ps"), 1)
                scores(0)
                scores(1)
                scores(2)
                transposes(0)
                for i in range(NT):
                    if i + 3 < NT:
                        scores(i + 3)
                    product(i)
                    if i + 1 < NT:
                        transposes(i + 1)

            def route(L, b):
                n = inst(L, b)
                for t in range(NT):
                    ins = mm(banks(6)[:, t * E:(t + 1) * E], xnT[:, t * P:(t + 1) * P], wT[:, 4, 0:E])
                ins.then_inc(sem("logits_ps"), 1)
                pe.wait_ge(sem("mask_ready"), n + 1)
                for t in range(NT):
                    ins = mm(ps[0:E, 0, 0:1], mask[:, t, :], onesb[:, 0:1], t == 0, t == NT - 1)
                ins.then_inc(sem("count_ps"), 1)
                for t in range(NT):
                    o = banks(7)[:, t * E:(t + 1) * E]
                    mm(o, before[:], mask[:, t, :], True, t == 0)
                    for k in range(t):
                        mm(o, onesb[:], mask[:, k, :], False, k == t - 1)
                pe.wait_ge(sem("tiles_ready"), n + 1)
                mm(ps[0:E, 1, 0:1], upto[0:E, 0:E], tls[:])
                mm(ps[:, 2, 0:E], tlsB[:], before[0:E, 0:E]).then_inc(sem("base_ps"), 1)
                pe.wait_ge(sem("ended_ready"), n + 1)
                mm(ps[0:1, 3, 0:P], onesb[0:E, 0:1], cmp[:]).then_inc(sem("expert_ps"), 1)

            def ffn(L, b):
                m = inst(L, b)
                G0 = m * GROUPS
                pe.wait_ge(sem("tile_experts"), m + 1)
                pe.wait_ge(sem("experts_loaded"), 16 * 8)
                regs = [nc.tensor.alloc_register(f"pe_expert{j}_{L}{b}") for j in range(GT)]

                def xT(g, r, late, k):
                    pe.wait_ge(sem(f"xg_loaded{r}"), 16 * (m * (GROUPS // RING) + k))
                    if late:
                        pe.wait_ge(sem("xgT_ready"), G0 + g - 1)
                    for j in range(GT):
                        ins = nc.tensor.transpose(banks(r % 2)[:, j * P:(j + 1) * P], xg[r][:, j, :], ident[:])
                    ins.then_inc(sem("xgT_ps"), 1)

                def hidden(g, r, late):
                    pe.wait_ge(sem("xgT_ready"), G0 + g + 1)
                    pe.wait_ge(sem("wk_ready"), G0 + g + 1)
                    if late:
                        pe.wait_ge(sem("hT_ready"), G0 + g - 1)
                    for j in range(GT):
                        ins = mm(banks(2 + r)[:, j * P:(j + 1) * P], wk[:, r, j, :], xgT[:, r, j * P:(j + 1) * P])
                    ins.then_inc(sem("h_ps"), 1)

                def outputs(g, r, late):
                    nc.tensor.reg_load(regs, tile_expert[0:1, b, bass.ds(g * GT, GT)])
                    pe.wait_ge(sem("hT_ready"), G0 + g + 1)
                    if late:
                        pe.wait_ge(sem("y_ready"), G0 + g - 1)
                    for j in range(GT):
                        e = pe.snap(regs[j], min_val=0, max_val=E - 1)
                        ins = mm(banks(4 + r)[:, j * D:(j + 1) * D], hT[:, r, j * P:(j + 1) * P],
                                 vals_sb[:, bass.ds(e, 1), :].rearrange("p a d -> p (a d)"))
                    ins.then_inc(sem("y_ps"), 1)
                for g in range(RING):
                    xT(g, g, g >= 2, 1)
                    if g >= 1:
                        hidden(g - 1, (g - 1) % 2, g >= 3)
                    if g >= 2:
                        outputs(g - 2, g % 2, False)
                with pe.Fori(1, GROUPS // RING) as i:
                    for r in range(RING):
                        xT(RING * i + r, r, True, i + 1)
                        hidden(RING * i + r - 1, (r - 1) % 2, True)
                        outputs(RING * i + r - 2, r % 2, True)
                hidden(GROUPS - 1, 1, True)
                outputs(GROUPS - 2, 0, True)
                outputs(GROUPS - 1, 1, True)
                for reg in regs:
                    nc.tensor.free_register(reg)

            def project_b(b):
                project(0, wqkv[:, 0:D]).then_inc(sem("b_proj_ps"), 1)
                project(2, wqkv[:, D:2 * D]).then_inc(sem("b_proj_ps"), 1)
                for t in range(NT):
                    ins = mm(banks(6, 2)[:, t * D:(t + 1) * D], xnT[:, t * P:(t + 1) * P], wqkv[:, 2 * D:3 * D])
                ins.then_inc(sem("b_proj_ps"), 1)

            def piece(U, k):
                hs, qt, c, w = PIECES[k]
                n = U * NP + k
                if k == 0:
                    pe.wait_ge(sem(f"qk_loaded{U % QRING}"), 16 * LOADS * (U // QRING + 1))
                if n >= 2:
                    pe.wait_ge(sem("max_read"), n - 1)
                diag = c == qt * P // W
                for i, h in enumerate(hs):
                    o = banks(5 + n % 2)[:, i * w:(i + 1) * w]
                    ins = mm(o, qst[U % QRING][:, h, qt * P:(qt + 1) * P], kst[U % QRING][:, h, c * W:c * W + w], True, not diag)
                    if diag:
                        ins = mm(o[:, w - P:w], identb[:], mask_qk[:], False, True)
                ins.then_inc(sem("max_ps"), 1)

            bank7 = {"maxT": 0, "avT": 0}

            def bank7_free():
                if bank7["maxT"]:
                    pe.wait_ge(sem("max_parts"), bank7["maxT"])
                if bank7["avT"]:
                    pe.wait_ge(sem("att_ready"), bank7["avT"])

            def maxT(U):
                pe.wait_ge(sem("max_ready"), U + 1)
                bank7_free()
                nc.tensor.transpose(ps[0:HG * NT, 7, 0:P], mxp[:, 0].rearrange("p h t -> p (h t)"), ident[:]).then_inc(sem("maxT_ps"), 1)
                bank7["maxT"] += 1

            def first_maxima():
                for k in range(NP):
                    piece(0, k)
                maxT(0)

            def score(U, s, j, hs):
                n = U * NCH + chunks_before(s) + j
                if s == 0 and j == 0:
                    pe.wait_ge(sem(f"max_loaded{U % QRING}"), 16 * PARTS * (U // QRING + 1))
                if n >= 2:
                    pe.wait_ge(sem("b_exp"), n - 1)
                c, kt = STEPS[s]
                q0, w = step_cols(s)
                diag = kt * P >= c * W
                for i, h in enumerate(hs):
                    k = i % in_bank(w)
                    o = banks(2 * (n % 2) + i // in_bank(w))[:, k * w:(k + 1) * w]
                    ins = mm(o, kst[U % QRING][:, h, kt * P:(kt + 1) * P], qst[U % QRING][:, h, q0:q0 + w], True, not diag)
                    if diag:
                        ins = mm(o[:, 0:P], identb[:], mask_kq[:], False, True)
                ins.then_inc(sem("scores_issued"), 1)

            def weigh(U, s):
                b, u = divmod(U, UNITS)
                c, kt = STEPS[s]
                q0, w = step_cols(s)
                pe.wait_ge(sem("b_exp"), U * NCH + chunks_before(s + 1))
                if kt == 0:
                    k = U * len(LAST) + sum(e < s for e in LAST)
                    if k:
                        pe.wait_ge(sem("av_ready"), k)
                for h in range(HG):
                    ins = mm(ps[32 * h:32 * h + DH + 1, 4, q0 - c * W:q0 - c * W + w], vaug[:, b, kt, u * HG + h, :],
                             pex[:, s % 2, h * w:(h + 1) * w], kt == 0, s in LAST, tile_position=(0, 32 * h), skip_group_check=True)
                ins.then_inc(sem("pv_done"), 1)

            def units(b):
                for t in range(UNITS * NS + 4):
                    u, s = divmod(t, NS)
                    U = b * UNITS + u
                    feeds = u < UNITS and U + 1 < ALL
                    ks = pieces_of(s) if feeds else range(0)
                    groups = chunks(s) if u < UNITS else []
                    parts = len(groups) + 1
                    for j in range(parts):
                        if j < len(groups):
                            score(U, s, j, groups[j])
                        elif 1 <= t <= UNITS * NS:
                            weigh(b * UNITS + (t - 1) // NS, (t - 1) % NS)
                        for k in ks[j * len(ks) // parts:(j + 1) * len(ks) // parts]:
                            piece(U + 1, k)
                    e = t - 3
                    if 0 <= e < UNITS * NS and e % NS in LAST:
                        pe.wait_ge(sem("av_ready"), (b * UNITS + e // NS) * len(LAST) + LAST.index(e % NS) + 1)
                        bank7_free()
                        for k in range(W // P):
                            ins = nc.tensor.transpose(banks(7)[:, k * P:(k + 1) * P], av_sb[:, k * P:(k + 1) * P], ident[:])
                        ins.then_inc(sem("avT_ps"), 1)
                        bank7["avT"] += 1
                    if feeds and s == S_NEG + 1:
                        maxT(U + 1)
                pe.wait_ge(sem("att_ready"), (b + 1) * UNITS * len(LAST))
                for t in range(NT):
                    ins = nc.tensor.transpose(banks(0, 2)[:, t * P:(t + 1) * P], att[:, t, :], ident[:])
                ins.then_inc(sem("attT_ps"), 1)
                pe.wait_ge(sem("attT"), b + 1)
                for t in range(NT):
                    ins = mm(banks(2, 2)[:, t * D:(t + 1) * D], attT[:, t * P:(t + 1) * P], wout[:])
                ins.then_inc(sem("b_out_ps"), 1)

            for i, (kind, L, b) in enumerate(PHASES):
                enter(pe, "pe", i)
                if kind in "apr":
                    norm(norm_no(i), b)
                {"a": lambda: attn_a(b), "p": lambda: project_b(b), "m": lambda: first_maxima(), "u": lambda: units(b),
                 "r": lambda: route(L, b), "f": lambda: ffn(L, b), "c": lambda: None}[kind]()
                pe.drain().then_inc(leave("pe"), 1)


_INS = ['L0_attn_a_x', 'L0_attn_a_Wq', 'L0_attn_a_bq', 'L0_attn_a_Wk', 'L0_attn_a_bk', 'L0_attn_a_Wv', 'L0_attn_a_bv',
        'L0_attn_a_Wo', 'L0_attn_a_bo', 'L0_attn_b_w_qkv', 'L0_attn_b_b_qkv', 'L0_attn_b_w_out', 'L0_attn_b_b_out',
        'L0_ffn_expert_sel', 'L0_ffn_keys', 'L0_ffn_values']


def kernel(**inputs):
    import numpy as _np
    import concourse.bacc as _bacc
    from concourse import mybir as _mybir
    from concourse.bass_utils import run_bass_kernel_spmd as _run

    nc = _bacc.Bacc("TRN2", target_bir_lowering=False, num_devices=1)
    arrays, args = {}, []
    for name in _INS:
        a = _np.ascontiguousarray(inputs[name])
        arrays[f"in_{name}"] = a
        args.append(nc.dram_tensor(f"in_{name}", a.shape, _mybir.dt.from_np(a.dtype), kind="ExternalInput").ap())
    o = nc.dram_tensor("out_x", inputs['L0_attn_a_x'].shape, _mybir.dt.float32, kind="ExternalOutput").ap()
    hybrid_kernel(nc, *args, o)
    r = _run(nc, [arrays], core_ids=[0])
    return r.results[0]["out_x"]
```
